# Optimizing a Trainium2 kernel written in Bass

```python
import numpy as np
import jax
import jax.numpy as jnp

def _softmax(x, axis=-1):
    return jax.nn.softmax(x, axis=axis)

def _gelu(x):
    return jax.nn.gelu(x, approximate=True)

def _silu(x):
    return jax.nn.silu(x)

def _sigmoid(x):
    return jax.nn.sigmoid(x)

def _layernorm(x, axis=-1, eps=1e-05):
    m = jnp.mean(x, axis=axis, keepdims=True)
    v = jnp.var(x, axis=axis, keepdims=True)
    return (x - m) / jnp.sqrt(v + eps)

def _scatter_add(tgt, idx, src, axis=0):
    return tgt.at[idx].add(src)

def _segment_sum(src, seg, n):
    return jax.ops.segment_sum(src, seg, n)
kernel_name = 'mk_adaln_d2_jaxref_r8_d89cf4'

def setup_inputs(seed: int=0):
    np.random.seed(seed)
    _w = jnp.asarray

    def _L0_attn_setup():
        import jax, jax.numpy as jnp
        import numpy as np
        EPS = 1e-05
        key = jax.random.key(seed)
        ks = jax.random.split(key, 8)
        B, T, C, H = (2, 256, 128, 16)
        hs = C // H
        scale = 1.0 / np.sqrt(C)
        x = jax.random.normal(ks[0], (B, T, C), dtype=jnp.float32)
        wq1 = jax.random.normal(ks[1], (H, C, hs), dtype=jnp.float32) * scale
        wk1 = jax.random.normal(ks[2], (H, C, hs), dtype=jnp.float32) * scale
        wq2 = jax.random.normal(ks[3], (H, C, hs), dtype=jnp.float32) * scale
        wk2 = jax.random.normal(ks[4], (H, C, hs), dtype=jnp.float32) * scale
        wv = jax.random.normal(ks[5], (H, C, hs), dtype=jnp.float32) * scale
        ln_gamma = jnp.ones((C,), dtype=jnp.float32)
        ln_beta = jnp.zeros((C,), dtype=jnp.float32)
        lamb = jnp.float32(0.8)
        return {'x': x, 'wq1': wq1, 'wk1': wk1, 'wq2': wq2, 'wk2': wk2, 'wv': wv, 'ln_gamma': ln_gamma, 'ln_beta': ln_beta, 'lamb': lamb}
    _L0_attn_in = _L0_attn_setup()

    def _L0_ffn_setup():
        import jax, jax.numpy as jnp
        import numpy as np
        N_EXPERTS = 16
        TOPK = 2
        CAPACITY_FACTOR = 1.0
        EPS_GATE = 1e-06
        LN_EPS = 1e-05
        key = jax.random.key(seed)
        ks = jax.random.split(key, 8)
        B, S, D, F, E = (4, 256, 128, 512, N_EXPERTS)
        Fp = F // E
        s = 0.02
        return {'x': jax.random.normal(ks[0], (B, S, D), dtype=jnp.float32), 'wg': s * jax.random.normal(ks[1], (D, E), dtype=jnp.float32), 'bg': jnp.zeros((E,), dtype=jnp.float32), 'w1': s * jax.random.normal(ks[2], (E, D, Fp), dtype=jnp.float32), 'b1': jnp.zeros((E, Fp), dtype=jnp.float32), 'w2': s * jax.random.normal(ks[3], (E, Fp, D), dtype=jnp.float32), 'b2': jnp.zeros((E, D), dtype=jnp.float32), 'gamma': jnp.ones((D,), dtype=jnp.float32), 'beta': jnp.zeros((D,), dtype=jnp.float32)}
    _L0_ffn_in = _L0_ffn_setup()
    _L0_c = _w((lambda *s: np.random.randn(*s).astype(np.float32) * 0.05)(8, 128))
    _L0_wmod = _w((lambda *s: np.random.randn(*s).astype(np.float32) * 0.05)(128, 6 * 128) * 128 ** (-0.5))

    def _L1_attn_setup():
        import jax, jax.numpy as jnp
        import numpy as np
        D_MODEL = 128
        N_HEADS = 16
        HEAD_DIM = D_MODEL // N_HEADS
        D_LATENT = 32
        LAMBDA_DECAY = 0.01
        TIME_STEP = 0.01
        CLAMP = 10000.0

        def _reference_tuple_inner(x, Wq, Wk, Wv, Wo, W_down_kv, W_up_k, W_up_v):
            B, S, _ = x.shape
            q = x @ Wq
            k = x @ Wk
            v = x @ Wv
            latent_kv = (k + v) @ W_down_kv
            k_rec = latent_kv @ W_up_k
            v_rec = latent_kv @ W_up_v

            def heads(t):
                return t.reshape(B, S, N_HEADS, HEAD_DIM).transpose(0, 2, 1, 3)
            qh, kh, vh = (heads(q), heads(k_rec), heads(v_rec))
            scale = 1.0 / (jnp.sqrt(jnp.float32(D_MODEL)) + 1e-08)
            scores = jnp.einsum('bhqd,bhkd->bhqk', qh, kh) * scale
            scores = jnp.clip(jnp.nan_to_num(scores, nan=-1000000000.0), -CLAMP, CLAMP)
            idx = jnp.arange(S, dtype=jnp.float32)
            decay = jnp.exp(-LAMBDA_DECAY * TIME_STEP * jnp.abs(idx[:, None] - idx[None, :]))
            scores = scores * decay[None, None, :, :]
            scores = jnp.clip(jnp.nan_to_num(scores, nan=-1000000000.0), -CLAMP, CLAMP)
            attn = jax.nn.softmax(scores, axis=-1)
            out = jnp.einsum('bhqk,bhkd->bhqd', attn, vh)
            out = out.transpose(0, 2, 1, 3).reshape(B, S, D_MODEL)
            return (out @ Wo, latent_kv)
        key = jax.random.key(seed)
        ks = jax.random.split(key, 8)
        B, S = (2, 256)

        def w(k, i, o):
            return jax.random.normal(k, (i, o), dtype=jnp.float32) * 0.02
        return {'x': jax.random.normal(ks[0], (B, S, D_MODEL), dtype=jnp.float32), 'Wq': w(ks[1], D_MODEL, D_MODEL), 'Wk': w(ks[2], D_MODEL, D_MODEL), 'Wv': w(ks[3], D_MODEL, D_MODEL), 'Wo': w(ks[4], D_MODEL, D_MODEL), 'W_down_kv': w(ks[5], D_MODEL, D_LATENT), 'W_up_k': w(ks[6], D_LATENT, D_MODEL), 'W_up_v': w(ks[7], D_LATENT, D_MODEL)}
    _L1_attn_in = _L1_attn_setup()

    def _L1_ffn_setup():
        import jax, jax.numpy as jnp
        import numpy as np
        D = 128
        H = 256
        E = 8
        TOP_K = 2
        N_SHARED = 1
        B, S = (2, 128)
        key = jax.random.key(seed)
        ks = jax.random.split(key, 12)
        sc = 0.02
        return {'hidden': jax.random.normal(ks[0], (B, S, D), jnp.float32), 'router_w': jax.random.normal(ks[1], (D, E), jnp.float32) * sc, 'router_b': jnp.zeros((E,), jnp.float32), 'sw1': jax.random.normal(ks[2], (D, H), jnp.float32) * sc, 'sb1': jnp.zeros((H,), jnp.float32), 'sw2': jax.random.normal(ks[3], (H, D), jnp.float32) * sc, 'sb2': jnp.zeros((D,), jnp.float32), 'rw1': jax.random.normal(ks[4], (E, D, H), jnp.float32) * sc, 'rb1': jnp.zeros((E, H), jnp.float32), 'rw2': jax.random.normal(ks[5], (E, H, D), jnp.float32) * sc, 'rb2': jnp.zeros((E, D), jnp.float32)}
    _L1_ffn_in = _L1_ffn_setup()
    _L1_c = _w((lambda *s: np.random.randn(*s).astype(np.float32) * 0.05)(8, 128))
    _L1_wmod = _w((lambda *s: np.random.randn(*s).astype(np.float32) * 0.05)(128, 6 * 128) * 128 ** (-0.5))
    _d = {'L0_attn_x': _L0_attn_in['x'], 'L0_attn_wq1': _L0_attn_in['wq1'], 'L0_attn_wk1': _L0_attn_in['wk1'], 'L0_attn_wq2': _L0_attn_in['wq2'], 'L0_attn_wk2': _L0_attn_in['wk2'], 'L0_attn_wv': _L0_attn_in['wv'], 'L0_attn_ln_gamma': _L0_attn_in['ln_gamma'], 'L0_attn_ln_beta': _L0_attn_in['ln_beta'], 'L0_attn_lamb': _L0_attn_in['lamb'], 'L0_ffn_wg': _L0_ffn_in['wg'], 'L0_ffn_bg': _L0_ffn_in['bg'], 'L0_ffn_w1': _L0_ffn_in['w1'], 'L0_ffn_b1': _L0_ffn_in['b1'], 'L0_ffn_w2': _L0_ffn_in['w2'], 'L0_ffn_b2': _L0_ffn_in['b2'], 'L0_ffn_gamma': _L0_ffn_in['gamma'], 'L0_ffn_beta': _L0_ffn_in['beta'], 'L0_c': _L0_c, 'L0_wmod': _L0_wmod, 'L1_attn_Wq': _L1_attn_in['Wq'], 'L1_attn_Wk': _L1_attn_in['Wk'], 'L1_attn_Wv': _L1_attn_in['Wv'], 'L1_attn_Wo': _L1_attn_in['Wo'], 'L1_attn_W_down_kv': _L1_attn_in['W_down_kv'], 'L1_attn_W_up_k': _L1_attn_in['W_up_k'], 'L1_attn_W_up_v': _L1_attn_in['W_up_v'], 'L1_ffn_router_w': _L1_ffn_in['router_w'], 'L1_ffn_router_b': _L1_ffn_in['router_b'], 'L1_ffn_sw1': _L1_ffn_in['sw1'], 'L1_ffn_sb1': _L1_ffn_in['sb1'], 'L1_ffn_sw2': _L1_ffn_in['sw2'], 'L1_ffn_sb2': _L1_ffn_in['sb2'], 'L1_ffn_rw1': _L1_ffn_in['rw1'], 'L1_ffn_rb1': _L1_ffn_in['rb1'], 'L1_ffn_rw2': _L1_ffn_in['rw2'], 'L1_ffn_rb2': _L1_ffn_in['rb2'], 'L1_c': _L1_c, 'L1_wmod': _L1_wmod}
    _x0 = _d['L0_attn_x']
    _d['L0_attn_x'] = jax.random.normal(jax.random.fold_in(jax.random.key(seed), 1), (8, 256, 128), dtype=_x0.dtype)
    del _x0
    return _d

def reference(L0_attn_x, L0_attn_wq1, L0_attn_wk1, L0_attn_wq2, L0_attn_wk2, L0_attn_wv, L0_attn_ln_gamma, L0_attn_ln_beta, L0_attn_lamb, L0_ffn_wg, L0_ffn_bg, L0_ffn_w1, L0_ffn_b1, L0_ffn_w2, L0_ffn_b2, L0_ffn_gamma, L0_ffn_beta, L0_c, L0_wmod, L1_attn_Wq, L1_attn_Wk, L1_attn_Wv, L1_attn_Wo, L1_attn_W_down_kv, L1_attn_W_up_k, L1_attn_W_up_v, L1_ffn_router_w, L1_ffn_router_b, L1_ffn_sw1, L1_ffn_sb1, L1_ffn_sw2, L1_ffn_sb2, L1_ffn_rw1, L1_ffn_rb1, L1_ffn_rw2, L1_ffn_rb2, L1_c, L1_wmod):

    def _L0_attn_ref(x, wq1, wk1, wq2, wk2, wv, ln_gamma, ln_beta, lamb):
        import jax, jax.numpy as jnp
        import numpy as np
        EPS = 1e-05
        B, T, C = x.shape
        H, _, hs = wq1.shape
        inv_sqrt_d = jnp.asarray(hs, x.dtype) ** (-0.5)
        q1 = jnp.einsum('btc,hcd->bhtd', x, wq1)
        k1 = jnp.einsum('btc,hcd->bhtd', x, wk1)
        q2 = jnp.einsum('btc,hcd->bhtd', x, wq2)
        k2 = jnp.einsum('btc,hcd->bhtd', x, wk2)
        v = jnp.einsum('btc,hcd->bhtd', x, wv)
        w1 = jax.nn.softmax(jnp.einsum('bhtd,bhsd->bhts', q1, k1) * inv_sqrt_d, axis=-1)
        w2 = jax.nn.softmax(jnp.einsum('bhtd,bhsd->bhts', q2, k2) * inv_sqrt_d, axis=-1)
        wei = w1 - lamb * w2
        out = jnp.einsum('bhts,bhsd->bhtd', wei, v)
        out = out.transpose(0, 2, 1, 3).reshape(B, T, H * hs)
        mu = out.mean(axis=-1, keepdims=True)
        var = out.var(axis=-1, keepdims=True)
        out = (out - mu) * jax.lax.rsqrt(var + EPS) * ln_gamma + ln_beta
        return (1.0 - lamb) * out

    def _L0_ffn_ref(x, wg, bg, w1, b1, w2, b2, gamma, beta):
        import jax, jax.numpy as jnp
        import numpy as np
        N_EXPERTS = 16
        TOPK = 2
        CAPACITY_FACTOR = 1.0
        EPS_GATE = 1e-06
        LN_EPS = 1e-05
        B, S, D = x.shape
        E = wg.shape[1]
        capacity = int(CAPACITY_FACTOR * B)
        scores = jax.nn.softmax(x @ wg + bg, axis=-1)
        _, top_i = jax.lax.top_k(scores, TOPK)
        mask = jax.nn.one_hot(top_i, E, dtype=scores.dtype).sum(-2)
        masked = scores * mask
        denom = masked.sum(0, keepdims=True) + EPS_GATE
        route = masked / denom * capacity
        route_e = jnp.transpose(route, (2, 0, 1))
        max_len = S // 2
        _, seq_ids = jax.lax.top_k(route_e, max_len)
        seq_ids = jnp.sort(seq_ids, axis=-1)
        b_idx = jnp.arange(B)[None, :, None]
        xg = x[b_idx, seq_ids]
        h = jnp.einsum('ebld,edf->eblf', xg, w1) + b1[:, None, None, :]
        h = jax.nn.gelu(h, approximate=False)
        out = jnp.einsum('eblf,efd->ebld', h, w2) + b2[:, None, None, :]
        outs = jnp.zeros_like(x).at[b_idx, seq_ids].add(out)
        z = x + outs
        mu = z.mean(-1, keepdims=True)
        var = ((z - mu) ** 2).mean(-1, keepdims=True)
        return (z - mu) / jnp.sqrt(var + LN_EPS) * gamma + beta

    def _L1_attn_ref(x, Wq, Wk, Wv, Wo, W_down_kv, W_up_k, W_up_v):
        import jax, jax.numpy as jnp
        import numpy as np
        D_MODEL = 128
        N_HEADS = 16
        HEAD_DIM = D_MODEL // N_HEADS
        D_LATENT = 32
        LAMBDA_DECAY = 0.01
        TIME_STEP = 0.01
        CLAMP = 10000.0

        def _reference_tuple_inner(x, Wq, Wk, Wv, Wo, W_down_kv, W_up_k, W_up_v):
            B, S, _ = x.shape
            q = x @ Wq
            k = x @ Wk
            v = x @ Wv
            latent_kv = (k + v) @ W_down_kv
            k_rec = latent_kv @ W_up_k
            v_rec = latent_kv @ W_up_v

            def heads(t):
                return t.reshape(B, S, N_HEADS, HEAD_DIM).transpose(0, 2, 1, 3)
            qh, kh, vh = (heads(q), heads(k_rec), heads(v_rec))
            scale = 1.0 / (jnp.sqrt(jnp.float32(D_MODEL)) + 1e-08)
            scores = jnp.einsum('bhqd,bhkd->bhqk', qh, kh) * scale
            scores = jnp.clip(jnp.nan_to_num(scores, nan=-1000000000.0), -CLAMP, CLAMP)
            idx = jnp.arange(S, dtype=jnp.float32)
            decay = jnp.exp(-LAMBDA_DECAY * TIME_STEP * jnp.abs(idx[:, None] - idx[None, :]))
            scores = scores * decay[None, None, :, :]
            scores = jnp.clip(jnp.nan_to_num(scores, nan=-1000000000.0), -CLAMP, CLAMP)
            attn = jax.nn.softmax(scores, axis=-1)
            out = jnp.einsum('bhqk,bhkd->bhqd', attn, vh)
            out = out.transpose(0, 2, 1, 3).reshape(B, S, D_MODEL)
            return (out @ Wo, latent_kv)
        return _reference_tuple_inner(x, Wq, Wk, Wv, Wo, W_down_kv, W_up_k, W_up_v)[0]

    def _L1_ffn_ref(hidden, router_w, router_b, sw1, sb1, sw2, sb2, rw1, rb1, rw2, rb2):
        import jax, jax.numpy as jnp
        import numpy as np
        D = 128
        H = 256
        E = 8
        TOP_K = 2
        N_SHARED = 1
        B, S = (2, 128)
        b, s, d = hidden.shape
        T = b * s
        flat = hidden.reshape(T, d)
        router_logits = flat @ router_w + router_b
        router_probs = jax.nn.softmax(router_logits, axis=-1)
        topk_probs, topk_idx = jax.lax.top_k(router_probs, TOP_K)
        weights = jnp.zeros_like(router_probs).at[jnp.arange(T)[:, None], topk_idx].add(topk_probs)
        sh = jax.nn.gelu(flat @ sw1 + sb1, approximate=False)
        shared_out = (sh @ sw2 + sb2) / N_SHARED
        h1 = jax.nn.gelu(jnp.einsum('td,edh->teh', flat, rw1) + rb1[None], approximate=False)
        expert_out = jnp.einsum('teh,ehd->ted', h1, rw2) + rb2[None]
        mixed = jnp.einsum('ted,te->td', expert_out, weights)
        return (shared_out + mixed).reshape(b, s, d)
    x = L0_attn_x
    mod = (_silu(L0_c) @ L0_wmod).reshape(L0_c.shape[0], 6, 1, -1)
    sa, ca, ga, sb, cb, gb = (mod[:, 0], mod[:, 1], mod[:, 2], mod[:, 3], mod[:, 4], mod[:, 5])
    ga = (2 * (ga >= 0) - 1) * jnp.maximum(jnp.abs(ga), 0.25)
    gb = (2 * (gb >= 0) - 1) * jnp.maximum(jnp.abs(gb), 0.25)
    h = _layernorm(x, axis=-1) * (1 + ca) + sa
    x = x + ga * _L0_attn_ref(h, L0_attn_wq1, L0_attn_wk1, L0_attn_wq2, L0_attn_wk2, L0_attn_wv, L0_attn_ln_gamma, L0_attn_ln_beta, L0_attn_lamb)
    h = _layernorm(x, axis=-1) * (1 + cb) + sb
    x = x + gb * _L0_ffn_ref(h, L0_ffn_wg, L0_ffn_bg, L0_ffn_w1, L0_ffn_b1, L0_ffn_w2, L0_ffn_b2, L0_ffn_gamma, L0_ffn_beta)
    mod = (_silu(L1_c) @ L1_wmod).reshape(L1_c.shape[0], 6, 1, -1)
    sa, ca, ga, sb, cb, gb = (mod[:, 0], mod[:, 1], mod[:, 2], mod[:, 3], mod[:, 4], mod[:, 5])
    ga = (2 * (ga >= 0) - 1) * jnp.maximum(jnp.abs(ga), 0.25)
    gb = (2 * (gb >= 0) - 1) * jnp.maximum(jnp.abs(gb), 0.25)
    h = _layernorm(x, axis=-1) * (1 + ca) + sa
    x = x + ga * _L1_attn_ref(h, L1_attn_Wq, L1_attn_Wk, L1_attn_Wv, L1_attn_Wo, L1_attn_W_down_kv, L1_attn_W_up_k, L1_attn_W_up_v)
    h = _layernorm(x, axis=-1) * (1 + cb) + sb
    x = x + gb * _L1_ffn_ref(h, L1_ffn_router_w, L1_ffn_router_b, L1_ffn_sw1, L1_ffn_sb1, L1_ffn_sw2, L1_ffn_sb2, L1_ffn_rw1, L1_ffn_rb1, L1_ffn_rw2, L1_ffn_rb2)
    return x

_drawn_inputs = setup_inputs


def setup_inputs(seed=0):
    import zlib

    import numpy as np

    out = dict(_drawn_inputs(seed))
    spreads = {'L0_attn_ln_gamma': (1.0, 0.6),
     'L0_attn_ln_beta': (0.0, 0.8),
     'L0_ffn_bg': (0.0, 0.297),
     'L0_ffn_b1': (0.0, 0.8),
     'L0_ffn_b2': (0.0, 0.1),
     'L0_ffn_gamma': (1.0, 0.2),
     'L0_ffn_beta': (0.0, 0.31),
     'L1_ffn_router_b': (0.0, 0.8),
     'L1_ffn_sb1': (0.0, 0.8),
     'L1_ffn_sb2': (0.0, 0.339),
     'L1_ffn_rb1': (0.0, 0.8),
     'L1_ffn_rb2': (0.0, 0.8)}
    factors = {'L0_ffn_w1': 6.332,
     'L0_ffn_w2': 5.679,
     'L1_attn_Wq': 8.0,
     'L1_attn_Wk': 8.0,
     'L1_attn_Wv': 8.0,
     'L1_attn_Wo': 8.0,
     'L1_attn_W_down_kv': 8.0,
     'L1_attn_W_up_k': 8.0,
     'L1_attn_W_up_v': 8.0,
     'L1_ffn_router_w': 8.0,
     'L1_ffn_sw1': 6.31,
     'L1_ffn_sw2': 5.676,
     'L1_ffn_rw1': 8.0,
     'L1_ffn_rw2': 8.0}
    for name, (base, spread) in spreads.items():
        noise = np.random.default_rng([zlib.crc32(name.encode()), seed]).standard_normal(out[name].shape)
        drawn = base * np.exp(spread * noise) if base else spread * noise
        out[name] = jnp.asarray(drawn.astype(out[name].dtype))
    for name, factor in factors.items():
        out[name] = (out[name] * factor).astype(out[name].dtype)
    return out
```

```python
import concourse.bass as bass
from concourse import mybir
from contextlib import ExitStack

F32 = mybir.dt.float32
F32R = mybir.dt.float32r
BF16 = mybir.dt.bfloat16
ALU = mybir.AluOpType
ACT = mybir.ActivationFunctionType
AX = mybir.AxisListType

B, T, C, H, HS = 8, 256, 128, 16, 8
NT = T // 128
G, J = 4, 4
E0, F0 = 16, 32
E1, F1 = 8, 256
NF0 = E0 * F0 // 128
NF1 = F1 // 128 + E1 * F1 // 128
EPS = 1e-5
CLAMP = 10000.0
SCALE0 = float(HS) ** -0.5
SCALE1 = 1.0 / (float(C) ** 0.5 + 1e-8)
ACC_STEPS = E1 + 3
W9_STEPS = 19

EARLY = [("ct", 2 * B), ("wmod0", 6 * C), ("wmod1", 6 * C), ("wqk0", 4 * C), ("wv0", C), ("ident", 128)]
LATE = [("wg", E0), ("w1", E0 * F0), ("b1", NF0), ("w2", NF0 * C), ("iota", E0), ("blocks", B),
        ("wq", C), ("wkt", C), ("wvt", C), ("wo", C), ("wdown", 32), ("router", E1),
        ("w1b", NF1 * 128), ("b1b", NF1), ("w2b", NF1 * C), ("decay", NT * T)]
ROWS = [("gammas", 4 * C), ("lamb", 1), ("bg", E0), ("rb", E1)]


def spans(parts):
    at, out = 0, {}
    for name, n in parts:
        out[name] = (at, at + n)
        at += n
    return out, at


EARLY_AT, N_EARLY = spans(EARLY)
LATE_AT, N_LATE = spans(LATE)
ROWS_AT, N_ROWS = spans(ROWS)


def ds(i, n=1):
    return bass.ds(i, n)


def build(nc, x, early, late, rows, b2, wup, rb2, out):
    ctx = ExitStack()
    with ctx:
        scope = [ctx]

        def sb(name, shape, dt=F32):
            return scope[0].enter_context(nc.sbuf_tensor(name, shape, dt))

        def new_scope():
            if scope[0] is not ctx:
                scope[0].close()
            scope[0] = ctx.enter_context(ExitStack())

        def sem(name):
            return ctx.enter_context(nc.semaphore(name))

        banks = [ctx.enter_context(nc.psum_tensor(f"bank{i}", [128, 512], F32)) for i in range(8)]
        ps_a, ps_b, ps_pv, ps_m = banks[0:2], banks[2:4], banks[4:6], banks[6:8]

        w_early = sb("w_early", [128, N_EARLY])
        w_late = sb("w_late", [128, N_LATE])
        w_rows = sb("w_rows", [1, N_ROWS])

        def we(name, a=0, n=None):
            lo, hi = EARLY_AT[name]
            return w_early[:, lo + a:hi if n is None else lo + a + n]

        def wl(name, a=0, n=None):
            lo, hi = LATE_AT[name]
            return w_late[:, lo + a:hi if n is None else lo + a + n]

        def wr(name):
            lo, hi = ROWS_AT[name]
            return w_rows[0:1, lo:hi]

        ident = we("ident")
        ones = sb("ones", [128, 512])
        zeros = sb("zeros", [8, 512])
        x_all = sb("x_all", [128, B * NT, C])
        h2t = sb("h2t", [128, B * T])
        silu = sb("silu", [128, 2 * B])
        silu_t = sb("silu_t", [128, 2 * B])
        mod_c = sb("mod_c", [128, 8, B])
        tab8 = sb("tab8", [8, 6, C])
        gate8 = sb("gate8", [8, 4, C])
        gpos = sb("gpos", [8, 4, C])
        gmax = sb("gmax", [8, 4, C])
        gam8 = sb("gam8", [8, 4, C])
        lam_c = sb("lam_c", [128, 2])
        tabs = sb("tabs", [128, B, 6, C])

        s_in = sem("early_loaded")
        s_xin = sem("x_loaded")
        s_late = sem("late_loaded")
        s_rows = sem("rows_loaded")
        s_const = sem("constants_set")
        s_set = sem("setup_vector")
        s_seta = sem("setup_scalar")
        s_setp = sem("setup_tensor")
        s_setg = sem("setup_gpsimd")

        spread = sb("spread", [128, 128 * F0], BF16)
        b2t = sb("b2t", [128, C])
        b2m = sb("b2m", [128, B, C])
        half = sb("half", [128, NT])
        eps_c = sb("eps_c", [128, NT])
        spare = sb("spare", [128, 64])

        vs = sb("vs", [128, NT, H, HS])
        v32 = sb("v32", [128, NT, H, 32])
        wup_s = sb("wup_s", [32, 2 * C])
        rb2_s = sb("rb2_s", [E1 + 1, C])
        s_small = sem("small_loaded")

        new_scope()
        stats = [sb(f"stats{i}", [128, NT, 6]) for i in range(3)]
        meanvar = [sb(f"meanvar{i}", [128, NT, 2]) for i in range(3)]
        rstd = [sb(f"rstd{i}", [128, NT]) for i in range(3)]
        xn1 = sb("xn1", [128, NT, C])
        ht = sb("ht", [128, T])
        hl = sb("hl", [128, 4, 2, T], F32R)
        stack = sb("stack", [128, G, 2, 2, T], F32R)
        negmax = sb("negmax", [128, G, 2, NT, J])
        mhl = sb("mhl", [128, G, 2 * NT, J, 2], F32R)
        mrow = sb("mrow", [8, G, 512], F32R)
        probs = sb("probs", [128, 2, J, NT * T])
        ot = sb("ot", [128, 2, 2 * T])
        ok = sb("ok", [128, G, 2, NT, J, HS + 1])
        rs = sb("rs", [128, G, 2, NT * J])
        prod = sb("prod", [128, G, 2, NT, J * HS])
        o_t = sb("o_t", [128, NT, C])
        on = sb("on", [128, NT, C])
        og = sb("og", [128, NT, C])
        ob = sb("ob", [128, NT, C])
        xc = sb("xc", [128, NT, C])
        xn2 = sb("xn2", [128, NT, C])

        s_a_full = sem("a_scores_done")
        s_a_max = sem("a_max_taken")
        s_b_full = sem("b_scores_done")
        s_exp = sem("exp_done")
        s_pv = sem("pv_done")
        s_ot = sem("pv_copied")
        s_otr = sem("pv_turned")
        s_ok = sem("pv_turned_copied")
        s_mhi = sem("max_high")
        s_mlo = sem("max_low")
        s_mtr = sem("max_turned")
        s_mcp = sem("max_turned_copied")
        s_st = [sem(f"stack_loaded{g}") for g in range(G)]
        s_mrow = [sem(f"max_rows_loaded{g}") for g in range(G)]
        s_ln = [[sem(f"ln{i}_{n}") for n in ("stats", "meanvar", "eps", "rstd", "normal")] for i in range(3)]
        s_xt = sem("x_turned")
        s_ht = sem("h_ready")
        s_q = sem("q_projected")
        s_k = sem("k_projected")
        s_v = sem("v_projected")
        s_qhi, s_khi, s_qlo, s_klo = sem("q_high"), sem("k_high"), sem("q_low"), sem("k_low")
        s_vs = sem("v_staged")
        s_vc = sem("v_spread")
        s_rc = sem("rowsum_inverse")
        s_pr = sem("o_scaled")
        s_o = sem("o_ready")
        s_og, s_ob, s_xc, s_xw = sem("o_gamma"), sem("o_beta"), sem("x_new"), sem("x_written")
        s_h2p = sem("h2_turned")
        s_h2 = sem("h2_ready")

        new_scope()
        lg = sb("lg", [128, B * NT, E0])
        sc = sb("sc", [128, B * NT, E0])
        key = sb("key", [128, B * NT, E0])
        eq = sb("eq", [128, B * NT, E0])
        pick = sb("pick", [128, B * NT, E0])
        col = [sb(f"col{i}", [128, B * NT]) for i in range(2)]
        rt = sb("rt", [128, NT, B, E0])
        den = sb("den", [128, NT * E0])
        route = sb("route", [128, T])
        top8 = sb("top8", [128, 8])
        sel = sb("sel", [128, T])
        selb = sb("selb", [128, T], BF16)
        h1 = sb("h1", [128, NF0, B * T])
        hm = sb("hm", [128, 2, NF0, T])
        h2c = sb("h2c", [128, 2, T])
        zn = sb("zn", [128, 2, NT, C])
        zg = sb("zg", [128, 2, NT, C])
        zb = sb("zb", [128, 2, NT, C])
        zst = sb("zst", [128, 2, NT, 6])
        zmv = sb("zmv", [128, 2, NT, 2])
        zrs = sb("zrs", [128, 2, NT])
        s_b2 = sem("b2_loaded")
        s_lg = sem("logits_done")
        s_r = sem("routing_vector")
        s_rexp = sem("routing_exp")
        s_rt = sem("route_turned")
        s_rtc = sem("route_turned_copied")
        s_g = sem("hidden_done")
        s_ge = sem("gelu_done")
        s_gs = sem("routing_gpsimd")
        s_mask = sem("mask_done")
        s_hm = sem("hidden_masked")
        s_z = sem("z_done")
        s_zst, s_zmv, s_zeps, s_zrs, s_zn = (sem(f"z_{n}") for n in ("stats", "meanvar", "eps", "rstd", "normal"))
        s_h2c = sem("h2_copied")
        s_zg, s_zb, s_zx = sem("z_gamma"), sem("z_beta"), sem("z_added")

        new_scope()
        wkv = sb("wkv", [128, C])
        wlat = sb("wlat", [32, C])
        wrec = sb("wrec", [128, 2 * C])
        stats1 = [sb(f"stats1_{i}", [128, NT, 6]) for i in range(2)]
        meanvar1 = [sb(f"meanvar1_{i}", [128, NT, 2]) for i in range(2)]
        rstd1 = [sb(f"rstd1_{i}", [128, NT]) for i in range(2)]
        xn3 = sb("xn3", [128, NT, C])
        xn4 = sb("xn4", [128, NT, C])
        ht1 = sb("ht1", [128, T])
        hl1 = sb("hl1", [128, 4, T], F32R)
        stack1 = sb("stack1", [128, G, 2, T], F32R)
        clip = sb("clip", [128, 2, NT * T])
        dec = sb("dec", [128, 4, NT * T])
        negmax1 = sb("negmax1", [128, 4, NT])
        prob1 = sb("prob1", [128, 2, NT * T])
        probt = sb("probt", [128, 2, J, NT * T])
        ot1 = sb("ot1", [128, 2, 2 * T])
        ok1 = sb("ok1", [128, 2, 2, NT, J, HS + 1])
        rs1 = sb("rs1", [128, 2, 2, NT, J])
        o1 = sb("o1", [128, NT, C])
        o1t = sb("o1t", [128, T])
        yg = sb("yg", [128, NT, C])

        c_w = sem("weights_folded")
        c_wp = sem("weights_products")
        c_s, c_clip, c_mul, c_max = sem("scores1"), sem("clipped"), sem("decayed"), sem("max1")
        c_exp, c_pt, c_ev = sem("exp1"), sem("exp_turned"), sem("exp_turned_copied")
        c_pv = sem("pv1")
        c_ot, c_otr, c_ok = sem("pv1_copied"), sem("pv1_turned"), sem("pv1_turned_copied")
        c_ln = [[sem(f"ln1_{i}_{n}") for n in ("stats", "meanvar", "eps", "rstd", "normal")] for i in range(2)]
        c_xt, c_ht = sem("x1_turned"), sem("h1_ready")
        c_qk, c_qhi, c_khi, c_lo = sem("qk1"), sem("q1_high"), sem("k1_high"), sem("qk1_low")
        c_v, c_vs, c_vc = sem("v1"), sem("v1_staged"), sem("v1_spread")
        c_st = [sem(f"stack1_loaded{g}") for g in range(G)]
        c_rc, c_o, c_oT, c_ots = sem("inverse1"), sem("o1_ready"), sem("o1_turned"), sem("o1_turned_copied")
        c_y, c_yg, c_x = sem("y"), sem("y_gated"), sem("x3_ready")
        c_h4p, c_h4 = sem("h4_turned"), sem("h4_ready")

        new_scope()
        lg1 = sb("lg1", [128, B * NT, E1])
        sc1 = sb("sc1", [128, B * NT, E1])
        key1 = sb("key1", [128, B * NT, E1])
        eq1 = sb("eq1", [128, B * NT, E1])
        pick1 = sb("pick1", [128, B * NT, E1])
        cols1 = [sb(f"cols1_{i}", [128, B * NT]) for i in range(2)]
        w9 = sb("w9", [128, B * NT, E1 + 1])
        w9t = sb("w9t", [E1 + 1, B * T])
        w9c = sb("w9c", [E1 + 1, 2, T])
        hid = sb("hid", [128, 2, NF1, T])
        acc = sb("acc", [128, 2, 2, C])
        f_lg, f_r, f_exp = sem("logits1"), sem("routing1_vector"), sem("routing1_exp")
        f_wt, f_wtc = sem("weights_turned"), sem("weights_turned_copied")
        f_h, f_ge = sem("hidden1"), sem("gelu1")
        f_wc = sem("weights_batch")
        f_se = sem("second_layer")
        f_acc = sem("sum_steps")
        f_out = sem("out_written")

        def at(u, lag):
            return (u - lag, 0) if u >= lag else (u - lag + H, -1)

        ORDER_1 = [
            [("xT", 1, c_ht, 1, 0), ("v", 1, c_vs, 1, 0), ("oT", -1, c_ots, 1, 0), ("h4T", -1, c_h4, 1, 0)],
            [("t1", -1, c_ok, 2, 1), ("qk", 1, c_lo, 1, 0), ("y", -1, c_yg, 1, 0), ("t0", 0, c_ok, 2, 0)]]

        ORDER_M = [
            [("mT3", -1, s_mcp, 4, 3), ("mT0", 0, s_mcp, 4, 0), ("xT", 1, s_ht, 1, 0), ("mT1", 0, s_mcp, 4, 1),
             ("q", 1, s_qlo, 1, 0), ("mT2", 0, s_mcp, 4, 2), ("v", 1, s_vs, 1, 0)],
            [("oT1", -1, s_ok, 4, 1), ("oT2", -1, s_ok, 4, 2), ("oT3", -1, s_ok, 4, 3), ("k", 1, s_klo, 1, 0),
             ("oT0", 0, s_ok, 4, 0), ("h2T", -1, s_h2, 1, 0)]]

        def wait_emptied(pe, bank, name, b, orders=ORDER_M):
            order = orders[bank]
            at = [u[0] for u in order].index(name)
            for back in range(1, 2 * len(order)):
                k, it = (at - back) % len(order), b + (at - back) // len(order)
                _, off, s, per, which = order[k]
                if isinstance(it, int) and not 0 <= it + off < B:
                    continue
                pe.wait_ge(s, per * (it + off) + which + 1)
                return

        def has(b, off):
            return not isinstance(b, int) or 0 <= b + off < B

        def run_loop(eng, body, aside=lambda: None):
            body(-1)
            body(0)
            aside()
            body(1)
            with eng.Fori(2, B - 1) as b:
                body(b)
            body(B - 1)
            body(B)

        def ge(eng, s, value, least=1):
            if not isinstance(value, int) or value >= least:
                eng.wait_ge(s, value)

        def b_round(b, u):
            return (b - 1, -1, u + 4) if u < 4 else (b, 0, u - 4)

        def pv_round(b, u):
            return (b - 1, -1, u + 3) if u < 5 else (b, 0, u - 5)

        held = [0]

        def hold(eng):
            k = held[0] = held[0] + 1
            if eng is nc.vector:
                eng.memset(spare[:, k:k + 1], 0.0)
            else:
                eng.tensor_tensor(spare[:, k:k + 1], half[:, 0:1], half[:, 0:1], ALU.mult)

        block = ctx.enter_context(nc.Block())

        @block.sync
        def _(sp):
            sp.dma_start(w_early[:, :], early).then_inc(s_in, 16)
            sp.dma_start(x_all[:, :, :], x).then_inc(s_xin, 16)
            sp.dma_start(w_rows[:, :], rows).then_inc(s_rows, 16)
            sp.dma_start(w_late[:, :], late).then_inc(s_late, 16)
            for b in range(B):
                sp.dma_start(b2t[E0 * b:E0 * b + E0, :], b2).then_inc(s_b2, 16)
            sp.dma_start(wup_s[:, :], wup).then_inc(s_small, 16)
            sp.dma_start(rb2_s[:, :], rb2).then_inc(s_small, 16)
            sp.wait_ge(s_const, 4)
            for g in range(G):
                sp.dma_start(stack[3::16, g, 1, :, :].bitcast(F32),
                             ones[0:8, :].rearrange("p (w t) -> p w t", w=2)).then_inc(s_st[g], 16)

            def load_stack(b, g):
                if g == 0:
                    sp.wait_ge(s_klo, b + 1)
                    sp.wait_ge(s_qlo, b + 1)
                ge(sp, s_b_full, 32 * b - 24 + 8 * g)
                rows_g = slice(32 * g, 32 * g + 32)
                for part, src in ((0, hl[rows_g, 2:0:-1]), (1, hl[rows_g, 2:4]), (2, hl[rows_g, 0:2])):
                    sp.dma_start(stack[part::4, g, :, :, :].bitcast(F32), src.bitcast(F32)).then_inc(s_st[g], 16)
                sp.dma_start(stack[3::16, g, 0, :, :].bitcast(F32),
                             zeros[:, :].rearrange("p (w t) -> p w t", w=2)).then_inc(s_st[g], 16)

            def load_max(b, g):
                sp.wait_ge(s_mcp, 4 * b + g + 1)
                sp.dma_start(stack[3::16, g, 0, :, :].bitcast(F32),
                             mrow[:, g, :].rearrange("p (w t) -> p w t", w=2).bitcast(F32)).then_inc(s_mrow[g], 16)

            def body(b):
                if has(b, -1):
                    load_max(b - 1, 3)
                if has(b, 0):
                    load_stack(b, 2)
                    load_max(b, 0)
                    load_stack(b, 3)
                    load_max(b, 1)
                if has(b, 1):
                    load_stack(b + 1, 0)
                if has(b, 0):
                    load_max(b, 2)
                if has(b, 1):
                    load_stack(b + 1, 1)

            run_loop(sp, body)

            def load_stack1(b, g):
                if g == 0:
                    sp.wait_ge(c_lo, b + 1)
                ge(sp, c_s, 16 * b - 12 + 4 * g)
                rows_g = slice(32 * g, 32 * g + 32)
                for part, src in ((0, hl1[rows_g, 2:0:-1]), (1, hl1[rows_g, 2:4]), (2, hl1[rows_g, 0:2]),
                                  (3, hl1[rows_g, 0:4:3])):
                    sp.dma_start(stack1[part::4, g, :, :].bitcast(F32), src.bitcast(F32)).then_inc(c_st[g], 16)

            def body1(b):
                if has(b, 0):
                    load_stack1(b, 3)
                if has(b, 1):
                    for g in range(3):
                        load_stack1(b + 1, g)

            run_loop(sp, body1)
            with sp.Fori(0, B) as b:
                sp.wait_ge(f_acc, ACC_STEPS * NT * (b + 2))
                sp.dma_start(out[:, ds(NT * b, NT), :], x_all[:, ds(NT * b, NT), :]).then_inc(f_out, 16)
            sp.wait_ge(f_out, 16 * B)

        @block.gpsimd
        def _(gp):
            gp.memset(zeros[:, :], 0.0).then_inc(s_const, 1)
            gp.memset(ones[:, :], 1.0).then_inc(s_const, 1)
            gp.memset(half[:, :], -0.5).then_inc(s_setg, 1)
            gp.memset(eps_c[:, :], EPS).then_inc(s_setg, 1)
            gp.memset(v32[:, :, :, :], 0.0).then_inc(s_setg, 1)
            gp.wait_ge(s_setg, 3)
            gp.memset(v32[:, :, :, HS:HS + 1], 1.0).then_inc(s_setg, 1)
            gp.wait_ge(s_setg, 4)

            def inverse_std(i, b):
                gp.wait_ge(s_ln[i][1], b + 1)
                gp.tensor_tensor(rstd[i][:, :], meanvar[i][:, :, 1], eps_c[:, :], ALU.add).then_inc(s_ln[i][2], 1)
                gp.wait_ge(s_ln[i][2], b + 1)
                gp.tensor_tensor(rstd[i][:, :], rstd[i][:, :], half[:, :], ALU.pow).then_inc(s_ln[i][3], 1)

            def normalise(i, b, dst, src):
                gp.wait_ge(s_ln[i][3], b + 1)
                hold(gp)
                for t in range(NT):
                    ins = gp.tensor_scalar(dst[:, t, :], src[:, t, :], meanvar[i][:, t, 0:1], rstd[i][:, t:t + 1],
                                           ALU.subtract, ALU.mult)
                ins.then_inc(s_ln[i][4], 1)

            def spread_v(b, part):
                gp.wait_ge(s_vs, b + 1)
                ge(gp, s_pv, 8 * b - 4 + 4 * part)
                hold(gp)
                hh = slice(8 * part, 8 * part + 8)
                gp.tensor_copy(v32[:, :, hh, 0:HS], vs[:, :, hh, :]).then_inc(s_vc, 1)

            def body(b):
                if has(b, 1):
                    inverse_std(0, b + 1)
                if has(b, 0):
                    spread_v(b, 0)
                    spread_v(b, 1)
                if has(b, -1):
                    c = b - 1
                    gp.wait_ge(s_rc, 2 * c + 2)
                    ge(gp, s_o, c)
                    gp.tensor_tensor(prod[:, :, :, :, :].rearrange("p g w t (j d) -> p (g w t j) d", d=HS),
                                     ok[:, :, :, :, :, 0:HS].rearrange("p g w t j d -> p (g w t j) d"),
                                     rs[:, :, :, :].rearrange("p g w x -> p (g w x)").unsqueeze(2).broadcast_to(
                                         [128, G * 2 * NT * J, HS]), ALU.mult).then_inc(s_pr, 1)
                    gp.wait_ge(s_pr, c + 1)
                    ge(gp, s_ln[1][4], c)
                    gp.tensor_tensor(o_t[:, :, :].rearrange("p t (g x) -> p g t x", g=G), prod[:, :, 0, :, :],
                                     prod[:, :, 1, :, :], ALU.subtract).then_inc(s_o, 1)
                    inverse_std(1, c)
                    normalise(1, c, on, o_t)
                    gp.wait_ge(s_ln[1][4], c + 1)
                    gp.tensor_tensor(og[:, :, :], on[:, :, :], tabs[:, ds(c), 0, :].broadcast_to([128, NT, C]),
                                     ALU.mult).then_inc(s_og, 1)
                    gp.wait_ge(s_og, c + 1)
                    gp.tensor_tensor(ob[:, :, :], og[:, :, :], tabs[:, ds(c), 1, :].broadcast_to([128, NT, C]),
                                     ALU.add).then_inc(s_ob, 1)
                    gp.wait_ge(s_ob, c + 1)
                    ge(gp, s_ln[2][4], c)
                    ge(gp, s_xw, c)
                    gp.tensor_tensor(xc[:, :, :], ob[:, :, :], x_all[:, ds(NT * c, NT), :],
                                     ALU.add).then_inc(s_xc, 1)
                    gp.wait_ge(s_xc, c + 1)
                    hold(gp)
                    gp.tensor_copy(x_all[:, ds(NT * c, NT), :], xc[:, :, :]).then_inc(s_xw, 1)
                    inverse_std(2, c)
                    ge(gp, s_h2p, c)
                    normalise(2, c, xn2, xc)

            def routing_tables():
                gp.tensor_copy(spread[:, :].rearrange("p (r f) -> p r f", f=F0),
                               ident.unsqueeze(2).broadcast_to([128, 128, F0])).then_inc(s_gs, 1)
                gp.wait_ge(s_late, 16)
                gp.wait_ge(s_b2, 16 * B)
                for b in range(B):
                    ins = gp.tensor_scalar(b2m[:, b, :], b2t[:, :], wl("blocks", b, 1), None, ALU.mult)
                ins.then_inc(s_gs, 1)

            gp.wait_ge(s_xin, 16)
            gp.wait_ge(s_seta, 5)
            run_loop(gp, body, routing_tables)

            gp.wait_ge(s_h2, B)
            with gp.Fori(0, B // 2) as pair:
                b = 2 * pair
                for i in range(2):
                    gp.tensor_copy(h2c[:, i, :], h2t[:, ds(T * (b + i), T)]).then_inc(s_h2c, 1)
                for i in range(2):
                    gp.wait_ge(s_zmv, b + i + 1)
                    gp.tensor_tensor(zrs[:, i, :], zmv[:, i, :, 1], eps_c[:, :], ALU.add).then_inc(s_zeps, 1)
                    gp.wait_ge(s_zeps, b + i + 1)
                    gp.tensor_tensor(zrs[:, i, :], zrs[:, i, :], half[:, :], ALU.pow).then_inc(s_zrs, 1)
                for i in range(2):
                    gp.wait_ge(s_zn, b + i + 1)
                    gp.tensor_tensor(zg[:, i, :, :], zn[:, i, :, :], tabs[:, ds(b + i), 2, :].broadcast_to([128, NT, C]),
                                     ALU.mult).then_inc(s_zg, 1)
                    gp.wait_ge(s_zg, b + i + 1)
                    gp.tensor_tensor(zb[:, i, :, :], zg[:, i, :, :], tabs[:, ds(b + i), 3, :].broadcast_to([128, NT, C]),
                                     ALU.add).then_inc(s_zb, 1)
                    gp.wait_ge(s_zb, b + i + 1)
                    gp.tensor_tensor(x_all[:, ds(NT * (b + i), NT), :], x_all[:, ds(NT * (b + i), NT), :], zb[:, i, :, :],
                                     ALU.add).then_inc(s_zx, 1)

            def inverse_std1(i, b):
                gp.wait_ge(c_ln[i][1], b + 1)
                gp.tensor_tensor(rstd1[i][:, :], meanvar1[i][:, :, 1], eps_c[:, :], ALU.add).then_inc(c_ln[i][2], 1)
                gp.wait_ge(c_ln[i][2], b + 1)
                gp.tensor_tensor(rstd1[i][:, :], rstd1[i][:, :], half[:, :], ALU.pow).then_inc(c_ln[i][3], 1)

            def spread_v1(b, part):
                gp.wait_ge(c_vs, b + 1)
                ge(gp, c_pv, 4 * b - 2 + 2 * part)
                hold(gp)
                hh = slice(8 * part, 8 * part + 8)
                gp.tensor_copy(v32[:, :, hh, 0:HS], vs[:, :, hh, :]).then_inc(c_vc, 1)

            def body1(b):
                for u in range(H):
                    if has(b, 0):
                        n = 16 * b + u
                        gp.wait_ge(c_clip, n + 1)
                        ge(gp, c_exp, n - 3)
                        gp.tensor_tensor(dec[:, u % 4, :], clip[:, u % 2, :], wl("decay"), ALU.mult).then_inc(c_mul, 1)
                    if u == 0 and has(b, 1):
                        inverse_std1(0, b + 1)
                    if u == 4 and has(b, 0):
                        spread_v1(b, 0)
                    if u == 5 and has(b, 0):
                        spread_v1(b, 1)
                    if u == 6 and has(b, -1):
                        c = b - 1
                        gp.wait_ge(c_rc, c + 1)
                        ge(gp, c_oT, c)
                        for p in range(2):
                            for w in range(2):
                                g = 2 * p + w
                                ins = gp.tensor_tensor(
                                    o1[:, :, 32 * g:32 * g + 32].rearrange("p t (j d) -> p t j d", d=HS),
                                    ok1[:, p, w, :, :, 0:HS],
                                    rs1[:, p, w, :, :].unsqueeze(3).broadcast_to([128, NT, J, HS]), ALU.mult)
                        ins.then_inc(c_o, 1)
                    if u == 10 and has(b, -1):
                        c = b - 1
                        gp.wait_ge(c_yg, c + 1)
                        gp.tensor_tensor(x_all[:, ds(NT * c, NT), :], x_all[:, ds(NT * c, NT), :], yg[:, :, :],
                                         ALU.add).then_inc(c_x, 1)
                    if u == 11 and has(b, -1):
                        inverse_std1(1, b - 1)

            gp.wait_ge(s_zx, B)
            run_loop(gp, body1)
            gp.wait_ge(f_wtc, 4)
            for i in range(2):
                gp.tensor_copy(w9c[:, i, :], w9t[:, T * i:T * (i + 1)]).then_inc(f_wc, 1)
            with gp.Fori(1, B // 2) as pair:
                for i in range(2):
                    b = 2 * pair + i
                    gp.wait_ge(f_se, NT * (b - 1))
                    hold(gp)
                    gp.tensor_copy(w9c[:, i, :], w9t[:, ds(T * b, T)]).then_inc(f_wc, 1)

        @block.scalar
        def _(act):
            act.wait_ge(s_in, 16)
            nc.scalar.activation(silu_t[:, :], we("ct"), ACT.Exp, scale=-1.0).then_inc(s_seta, 1)
            for i in range(4):
                act.wait_ge(s_setp, 5 + i)
                b4 = 2 * i
                for k in range(2):
                    for n, (lo, hi) in enumerate(((0, 4), (4, 6))):
                        ins = nc.scalar.activation(tabs[:, b4 + k, lo:hi, :].rearrange("p a c -> p (a c)"),
                                                   [ps_a, ps_b][k][n][:, 0:(hi - lo) * C], ACT.Copy)
                ins.then_inc(s_seta, 1)

            def exp_fill(b, r, j):
                n = 32 * b + 4 * r + j
                act.wait_ge(s_b_full, n + 1)
                if j == 0:
                    ge(act, s_pv, 8 * b + r - 1)
                nc.scalar.activation(probs[:, r % 2, j, :], ps_b[j % 2][:, :], ACT.Exp,
                                     scale=SCALE0).then_inc(s_exp, 1)

            def copy_pv(b, g):
                act.wait_ge(s_pv, 8 * b + 2 * g + 2)
                ge(act, s_otr, 4 * b + g - 1)
                nc.scalar.activation(ot[:, g % 2, :], ps_pv[g % 2][:, :], ACT.Copy).then_inc(s_ot, 1)

            def copy_turned(b, g):
                act.wait_ge(s_otr, 4 * b + g + 1)
                if g == 0:
                    ge(act, s_pr, b)
                src = ps_m[1][:, :].rearrange("p (x j e) -> p x j e", j=J, e=32)[:, :, :, 0:HS + 1]
                nc.scalar.activation(ok[:, g, :, :, :, :].rearrange("p w t j d -> p (w t) j d"), src,
                                     ACT.Copy).then_inc(s_ok, 1)

            def copy_max(b, g):
                act.wait_ge(s_mtr, 4 * b + g + 1)
                ge(act, s_mrow[g], 16 * b)
                nc.scalar.activation(mrow[:, g, :], ps_m[0][0:8, :], ACT.Copy).then_inc(s_mcp, 1)

            def body(b):
                for u in range(8):
                    bb, off, r = b_round(b, u)
                    pb, poff, pr = pv_round(b, u)
                    for j in range(2):
                        if has(b, off):
                            exp_fill(bb, r, j)
                    if u == 0 and has(b, -1):
                        copy_max(b - 1, 3)
                    if u in (2, 4, 6) and has(b, 0):
                        copy_max(b, u // 2 - 1)
                    for j in range(2, 4):
                        if has(b, off):
                            exp_fill(bb, r, j)
                    if pr % 2 and has(b, poff):
                        copy_pv(pb, pr // 2)
                        copy_turned(pb, pr // 2)
                    if u == 2 and has(b, 1):
                        act.wait_ge(s_xt, b + 2)
                        ge(act, s_v, b + 1)
                        nc.scalar.activation(ht[:, :], ps_m[0][:, 0:T], ACT.Identity, scale=mod_c[:, 1, ds(b + 1)],
                                             bias=mod_c[:, 0, ds(b + 1)]).then_inc(s_ht, 1)
                    if u == 5 and has(b, 1):
                        act.wait_ge(s_q, b + 2)
                        for g in range(G):
                            ge(act, s_st[g], 64 * (b + 1) + 16, 17)
                        nc.scalar.activation(hl[:, 2, :, :].rearrange("p w t -> p (w t)"), ps_m[0][:, :],
                                             ACT.Copy).then_inc(s_qhi, 1)
                        act.wait_ge(s_k, b + 2)
                        nc.scalar.activation(hl[:, 1, :, :].rearrange("p w t -> p (w t)"), ps_m[1][:, :],
                                             ACT.Copy).then_inc(s_khi, 1)
                    if u == 6 and has(b, 1):
                        act.wait_ge(s_v, b + 2)
                        ge(act, s_vc, 2 * b + 2)
                        nc.scalar.activation(vs[:, :, :, :].rearrange("p t h d -> p (t h d)"), ps_m[0][:, 0:T],
                                             ACT.Copy).then_inc(s_vs, 1)
                    if u == 7 and has(b, -1):
                        act.wait_ge(s_h2p, b)
                        nc.scalar.activation(h2t[:, ds(T * (b - 1), T)], ps_m[1][:, 0:T], ACT.Identity,
                                             scale=mod_c[:, 3, ds(b - 1)], bias=mod_c[:, 2, ds(b - 1)]).then_inc(s_h2, 1)

            run_loop(act, body)

            act.wait_ge(s_r, 2)
            nc.scalar.activation(lg[:, :, :], lg[:, :, :], ACT.Exp).then_inc(s_rexp, 1)

            def gelu(n):
                f, c = n % NF0, n // NF0
                act.wait_ge(s_g, n + 1)
                nc.scalar.activation(h1[:, f, c * 512:(c + 1) * 512], ps_b[n % 2][:, :], ACT.Gelu,
                                     bias=wl("b1", f, 1)).then_inc(s_ge, 1)

            act.wait_ge(s_late, 16)
            for n in range(8):
                gelu(n)
            act.wait_ge(s_rt, 1)
            nc.scalar.activation(route[:, :], ps_a[1][:, 0:T], ACT.Copy).then_inc(s_rtc, 1)
            for n in range(8, 16):
                gelu(n)

            act.wait_ge(c_wp, 1)
            nc.scalar.activation(wlat[:, :], ps_a[0][0:32, 0:C], ACT.Copy).then_inc(c_w, 1)
            act.wait_ge(c_wp, 2)
            nc.scalar.activation(wrec[:, :], ps_a[1][:, 0:2 * C], ACT.Copy).then_inc(c_w, 1)

            def body1(b):
                for u in range(H):
                    h, off = at(u, 3)
                    if has(b, off):
                        n = 16 * (b + off) + h
                        act.wait_ge(c_max, n + 1)
                        ge(act, c_pt, n - 1)
                        for t in range(NT):
                            ins = nc.scalar.activation(prob1[:, h % 2, t * T:(t + 1) * T], dec[:, h % 4, t * T:(t + 1) * T],
                                                       ACT.Exp, bias=negmax1[:, h % 4, t:t + 1])
                        ins.then_inc(c_exp, 1)
                    h, off = at(u, 4)
                    if has(b, off):
                        n = 16 * (b + off) + h
                        act.wait_ge(c_pt, n + 1)
                        if h % 4 == 0:
                            ge(act, c_pv, 4 * (b + off) + h // 4 - 1)
                        nc.scalar.activation(probt[:, h // 4 % 2, h % 4, :], ps_b[h % 2][:, :],
                                             ACT.Copy).then_inc(c_ev, 1)
                    for p, tick, off in ((0, 12, 0), (1, 4, -1)):
                        if u == tick and has(b, off):
                            c = b + off
                            act.wait_ge(c_pv, 4 * c + 2 * p + 2)
                            ge(act, c_otr, 2 * c + p - 1)
                            nc.scalar.activation(ot1[:, p, :], ps_pv[p][:, :], ACT.Copy).then_inc(c_ot, 1)
                        if u == tick + 1 and has(b, off):
                            c = b + off
                            act.wait_ge(c_otr, 2 * c + p + 1)
                            if p == 0:
                                ge(act, c_o, c)
                            src = ps_m[1][:, :].rearrange("p (x j e) -> p x j e", j=J, e=32)[:, :, :, 0:HS + 1]
                            nc.scalar.activation(ok1[:, p, :, :, :, :].rearrange("p w t j d -> p (w t) j d"), src,
                                                 ACT.Copy).then_inc(c_ok, 1)
                    if u == 3 and has(b, 1):
                        act.wait_ge(c_xt, b + 2)
                        ge(act, c_v, b + 1)
                        nc.scalar.activation(ht1[:, :], ps_m[0][:, 0:T], ACT.Identity, scale=mod_c[:, 5, ds(b + 1)],
                                             bias=mod_c[:, 4, ds(b + 1)]).then_inc(c_ht, 1)
                    if u == 6 and has(b, 1):
                        act.wait_ge(c_qk, b + 2)
                        for g in range(G):
                            ge(act, c_st[g], 64 * (b + 1))
                        nc.scalar.activation(hl1[:, 2, :], ps_m[1][:, 0:T], ACT.Copy).then_inc(c_qhi, 1)
                        nc.scalar.activation(hl1[:, 1, :], ps_m[1][:, T:2 * T], ACT.Copy).then_inc(c_khi, 1)
                    if u == 7 and has(b, 1):
                        act.wait_ge(c_v, b + 2)
                        ge(act, c_vc, 2 * b + 2)
                        nc.scalar.activation(vs[:, :, :, :].rearrange("p t h d -> p (t h d)"), ps_m[0][:, 0:T],
                                             ACT.Copy).then_inc(c_vs, 1)
                    if u == 8 and has(b, -1):
                        act.wait_ge(c_oT, b)
                        ge(act, c_y, b - 1)
                        nc.scalar.activation(o1t[:, :], ps_m[0][:, 0:T], ACT.Copy).then_inc(c_ots, 1)
                    if u == 15 and has(b, -1):
                        act.wait_ge(c_h4p, b)
                        nc.scalar.activation(h2t[:, ds(T * (b - 1), T)], ps_m[0][:, 0:T], ACT.Identity,
                                             scale=mod_c[:, 7, ds(b - 1)], bias=mod_c[:, 6, ds(b - 1)]).then_inc(c_h4, 1)

            run_loop(act, body1)

            act.wait_ge(f_r, 2)
            nc.scalar.activation(lg1[:, :, :], lg1[:, :, :], ACT.Exp).then_inc(f_exp, 1)
            for i in range(4):
                act.wait_ge(f_wt, i + 1)
                nc.scalar.activation(w9t[:, 512 * i:512 * (i + 1)], ps_pv[i % 2][0:E1 + 1, :],
                                     ACT.Copy).then_inc(f_wtc, 1)

            def gelus(c, i, f2):
                n = 9 * c + f2
                act.wait_ge(f_h, n + 1)
                for k in range(2):
                    f = 2 * f2 + k
                    ins = nc.scalar.activation(hid[:, i, f, :], ps_b[(i + f2) % 2][:, k * T:(k + 1) * T], ACT.Gelu,
                                               bias=wl("b1b", f, 1))
                ins.then_inc(f_ge, 1)

            with act.Fori(0, B // 2) as pair:
                for i in range(2):
                    for f2 in range(NF1 // 2):
                        gelus(2 * pair + i, i, f2)

        @block.vector
        def _(dve):
            steps = [0]

            def link(ins):
                steps[0] += 1
                ins.then_inc(s_set, 1)
                dve.wait_ge(s_set, steps[0])

            nc.vector.memset(stack[:, 0:2, :, :, :].bitcast(F32), 0.0).then_inc(s_const, 1)
            nc.vector.memset(stack[:, 2:4, :, :, :].bitcast(F32), 0.0).then_inc(s_const, 1)
            dve.wait_ge(s_seta, 1)
            link(nc.vector.tensor_scalar(silu_t[:, :], silu_t[:, :], 1.0, None, ALU.add))
            link(nc.vector.reciprocal(silu_t[:, :], silu_t[:, :]))
            link(nc.vector.tensor_tensor(silu[:, :], silu_t[:, :], we("ct"), ALU.mult))
            dve.wait_ge(s_setp, 1)
            mods = ps_m[0][:, 0:8 * B].rearrange("p (k b) -> p k b", b=B)
            link(nc.vector.tensor_copy(mod_c[:, 0::2, :], mods[:, 0::2, :]))
            link(nc.vector.tensor_scalar(mod_c[:, 1::2, :], mods[:, 1::2, :], 1.0, None, ALU.add))
            dve.wait_ge(s_setp, 2)
            flat = lambda t: t[:, :, :].rearrange("p a c -> p (a c)")
            link(nc.vector.tensor_copy(flat(gate8), ps_m[1][0:8, :]))
            link(nc.vector.tensor_scalar(flat(gpos), flat(gate8), 0.0, None, ALU.is_ge))
            link(nc.vector.tensor_scalar(flat(gmax), flat(gate8), 0.25, None, ALU.max))
            link(nc.vector.tensor_tensor(flat(gmax), flat(gmax), flat(gpos), ALU.mult))
            link(nc.vector.tensor_scalar(flat(gate8), flat(gate8), -0.25, None, ALU.min))
            link(nc.vector.tensor_scalar(flat(gpos), flat(gpos), -1.0, 1.0, ALU.mult, ALU.add))
            link(nc.vector.tensor_tensor(flat(gate8), flat(gate8), flat(gpos), ALU.mult))
            link(nc.vector.tensor_tensor(flat(gate8), flat(gate8), flat(gmax), ALU.add))
            dve.wait_ge(s_setp, 4)
            link(nc.vector.tensor_copy(lam_c[:, 0:1], ps_m[0][:, 0:1]))
            link(nc.vector.tensor_scalar(lam_c[:, 1:2], lam_c[:, 0:1], -1.0, 1.0, ALU.mult, ALU.add))
            link(nc.vector.tensor_copy(flat(gam8), ps_a[0][0:8, :]))
            link(nc.vector.tensor_tensor(tab8[:, 0:2, :], gam8[:, 0:2, :], gate8[:, 0:1, :].broadcast_to([8, 2, C]),
                                         ALU.mult))
            link(nc.vector.tensor_scalar(tab8[:, 0:2, :], tab8[:, 0:2, :], lam_c[0:8, 1:2], None, ALU.mult))
            link(nc.vector.tensor_tensor(tab8[:, 2:4, :], gam8[:, 2:4, :], gate8[:, 1:2, :].broadcast_to([8, 2, C]),
                                         ALU.mult))
            link(nc.vector.tensor_copy(tab8[:, 4:6, :], gate8[:, 2:4, :]))
            assert steps[0] == 20

            def ln_stats(i, b, src):
                for t in range(NT):
                    ins = nc.vector.bn_stats(stats[i][:, t, :], src(t))
                ins.then_inc(s_ln[i][0], 1)
                dve.wait_ge(s_ln[i][0], b + 1)
                hold(dve)
                for t in range(NT):
                    ins = nc.vector.bn_aggr(meanvar[i][:, t, :], stats[i][:, t, :])
                ins.then_inc(s_ln[i][1], 1)

            def take_max(b, u, j):
                n = 32 * b + 4 * u + j
                dve.wait_ge(s_a_full, n + 1)
                nc.vector.tensor_reduce(negmax[:, u // 2, u % 2, :, j],
                                        ps_a[j % 2][:, :].rearrange("p (t k) -> p t k", t=NT), AX.X, ALU.max,
                                        negate=True).then_inc(s_a_max, 1)

            def split_max(b, g):
                dve.wait_ge(s_a_max, 32 * b + 8 * g + 8)
                ge(dve, s_mtr, 4 * b + g - 3)
                src = negmax[:, g, :, :, :].rearrange("p w t j -> p (w t) j")
                nc.vector.tensor_copy(mhl[:, g, :, :, 0], src).then_inc(s_mhi, 1)
                dve.wait_ge(s_mhi, 4 * b + g + 1)
                nc.vector.tensor_tensor(mhl[:, g, :, :, 1], src, mhl[:, g, :, :, 0].bitcast(F32),
                                        ALU.subtract).then_inc(s_mlo, 1)

            def low_part(bank, hi, lo):
                nc.vector.tensor_tensor(hl[:, lo, :, :].rearrange("p w t -> p (w t)"), ps_m[bank][:, :],
                                        hl[:, hi, :, :].rearrange("p w t -> p (w t)").bitcast(F32),
                                        ALU.subtract).then_inc([s_qlo, s_klo][bank], 1)

            def body(b):
                for u in range(8):
                    if has(b, 0):
                        for j in range(4):
                            take_max(b, u, j)
                        if u % 2:
                            split_max(b, u // 2)
                    if u == 0 and has(b, 1):
                        ge(dve, s_ln[0][4], b + 1)
                        ln_stats(0, b + 1, lambda t: x_all[:, ds(NT * (b + 1) + t), :].rearrange("p a c -> p (a c)"))
                    if u == 1 and has(b, 1):
                        dve.wait_ge(s_ln[0][3], b + 2)
                        ge(dve, s_xt, b + 1)
                        for t in range(NT):
                            ins = nc.vector.tensor_scalar(xn1[:, t, :].unsqueeze(1), x_all[:, ds(NT * (b + 1) + t), :],
                                                          meanvar[0][:, t, 0:1], rstd[0][:, t:t + 1], ALU.subtract,
                                                          ALU.mult)
                        ins.then_inc(s_ln[0][4], 1)
                    if u == 4 and has(b, -1):
                        c = b - 1
                        dve.wait_ge(s_ok, 4 * c + 4)
                        ge(dve, s_pr, c)
                        nc.vector.reciprocal(rs[:, :, :, :].rearrange("p g w x -> p (g w x)"),
                                             ok[:, :, :, :, :, HS].rearrange("p g w t j -> p (g w t j)")
                                             ).then_inc(s_rc, 1)
                        dve.wait_ge(s_rc, 2 * c + 1)
                        nc.vector.tensor_scalar(rs[:, :, 1, :], rs[:, :, 1, :], lam_c[:, 0:1], None,
                                                ALU.mult).then_inc(s_rc, 1)
                    if u == 5 and has(b, 1):
                        dve.wait_ge(s_qhi, b + 2)
                        low_part(0, 2, 0)
                        dve.wait_ge(s_khi, b + 2)
                        low_part(1, 1, 3)
                    if u == 6 and has(b, -1):
                        dve.wait_ge(s_o, b)
                        ge(dve, s_ln[1][4], b - 1)
                        ln_stats(1, b - 1, lambda t: o_t[:, t, :])
                    if u == 7 and has(b, -1):
                        dve.wait_ge(s_xc, b)
                        ge(dve, s_ln[2][4], b - 1)
                        ln_stats(2, b - 1, lambda t: xc[:, t, :])

            dve.wait_ge(s_xin, 16)
            run_loop(dve, body)

            steps[0] = 0

            def step(ins):
                steps[0] += 1
                ins.then_inc(s_r, 1)
                dve.wait_ge(s_r, steps[0])

            over = lambda t: t[:, :].unsqueeze(2).broadcast_to([128, B * NT, E0])
            flat2 = lambda t: t[:, :, :].rearrange("p a e -> p (a e)")
            iota = wl("iota").unsqueeze(1).broadcast_to([128, B * NT, E0])
            dve.wait_ge(s_lg, 1)
            logits = ps_a[0][:, 0:B * NT * E0].rearrange("p (a e) -> p a e", e=E0)
            step(nc.vector.tensor_reduce(col[0][:, :], logits, AX.X, ALU.max))
            step(nc.vector.tensor_tensor(lg[:, :, :], logits, over(col[0]), ALU.subtract))
            dve.wait_ge(s_rexp, 1)
            dve.wait_ge(s_late, 16)
            step(nc.vector.tensor_reduce(col[0][:, :], lg[:, :, :], AX.X, ALU.add))
            step(nc.vector.reciprocal(col[0][:, :], col[0][:, :]))
            step(nc.vector.tensor_tensor(lg[:, :, :], lg[:, :, :], over(col[0]), ALU.mult))
            for k in range(2):
                src = [lg, sc][k]
                step(nc.vector.tensor_reduce(col[0][:, :], src[:, :, :], AX.X, ALU.max))
                step(nc.vector.tensor_tensor(eq[:, :, :], src[:, :, :], over(col[0]), ALU.is_equal))
                step(nc.vector.scalar_tensor_tensor(key[:, :, :], eq[:, :, :], -64.0, iota, ALU.mult, ALU.add))
                step(nc.vector.tensor_reduce(col[1][:, :], key[:, :, :], AX.X, ALU.min))
                step(nc.vector.tensor_tensor([pick, eq][k][:, :, :], key[:, :, :], over(col[1]), ALU.is_equal))
                if k == 0:
                    step(nc.vector.scalar_tensor_tensor(flat2(sc), flat2(pick), -4.0, flat2(lg), ALU.mult, ALU.add))
            step(nc.vector.tensor_tensor(flat2(pick), flat2(pick), flat2(eq), ALU.add))
            step(nc.vector.tensor_tensor(flat2(pick), flat2(pick), flat2(lg), ALU.mult))
            step(nc.vector.tensor_reduce(den[:, :], pick[:, :, :].rearrange("p (b t) e -> p (t e) b", t=NT), AX.X,
                                         ALU.add))
            step(nc.vector.tensor_scalar(den[:, :], den[:, :], 1e-6, None, ALU.add))
            step(nc.vector.reciprocal(den[:, :], den[:, :]))
            step(nc.vector.tensor_scalar(den[:, :], den[:, :], float(B), None, ALU.mult))
            step(nc.vector.tensor_tensor(rt[:, :, :, :].rearrange("p t b e -> p b t e"),
                                         pick[:, :, :].rearrange("p (b t) e -> p b t e", t=NT),
                                         den[:, :].rearrange("p (t e) -> p t e", e=E0).unsqueeze(1).broadcast_to(
                                             [128, B, NT, E0]), ALU.mult))
            n_route = steps[0]
            assert n_route == 23, n_route
            dve.wait_ge(s_rtc, 1)
            for k in range(T // 2 // 8):
                step(nc.vector.max(top8[:, :], route[:, :]))
                step(nc.vector.match_replace(out=route[:, :], in_to_replace=top8[:, :], in_values=route[:, :],
                                             imm_value=-1.0))
            step(nc.vector.tensor_scalar(selb[:, :], route[:, :], -1.0, None, ALU.is_equal))
            step(nc.vector.tensor_scalar(sel[:, :], route[:, :], -1.0, None, ALU.is_equal))

            dve.wait_ge(s_ge, 16)
            with dve.Fori(0, B // 2) as pair:
                b = 2 * pair
                for i in range(2):
                    dve.wait_ge(s_mask, b + i + 1)
                    for f in range(0, NF0, 2):
                        ins = nc.vector.tensor_tensor(hm[:, i, f:f + 2, :], h1[:, f:f + 2, ds(T * (b + i), T)],
                                                      [ps_a, ps_b][i][f // 2][:, :].rearrange("p (f t) -> p f t", f=2),
                                                      ALU.mult)
                    ins.then_inc(s_hm, 1)
                for i in range(2):
                    dve.wait_ge(s_z, b + i + 1)
                    for t in range(NT):
                        ins = nc.vector.bn_stats(zst[:, i, t, :], ps_pv[i][:, t * C:(t + 1) * C])
                    ins.then_inc(s_zst, 1)
                    dve.wait_ge(s_zst, b + i + 1)
                    hold(dve)
                    for t in range(NT):
                        ins = nc.vector.bn_aggr(zmv[:, i, t, :], zst[:, i, t, :])
                    ins.then_inc(s_zmv, 1)
                for i in range(2):
                    dve.wait_ge(s_zrs, b + i + 1)
                    for t in range(NT):
                        ins = nc.vector.tensor_scalar(zn[:, i, t, :], ps_pv[i][:, t * C:(t + 1) * C],
                                                      zmv[:, i, t, 0:1], zrs[:, i, t:t + 1], ALU.subtract, ALU.mult)
                    ins.then_inc(s_zn, 1)

            nc.vector.tensor_tensor(wkv[:, :], wl("wkt"), wl("wvt"), ALU.add).then_inc(c_w, 1)

            def ln_stats1(i, b):
                for t in range(NT):
                    ins = nc.vector.bn_stats(stats1[i][:, t, :],
                                             x_all[:, ds(NT * b + t), :].rearrange("p a c -> p (a c)"))
                ins.then_inc(c_ln[i][0], 1)
                dve.wait_ge(c_ln[i][0], b + 1)
                hold(dve)
                for t in range(NT):
                    ins = nc.vector.bn_aggr(meanvar1[i][:, t, :], stats1[i][:, t, :])
                ins.then_inc(c_ln[i][1], 1)

            def normalise1(i, b, dst):
                dve.wait_ge(c_ln[i][3], b + 1)
                for t in range(NT):
                    ins = nc.vector.tensor_scalar(dst[:, t, :].unsqueeze(1), x_all[:, ds(NT * b + t), :],
                                                  meanvar1[i][:, t, 0:1], rstd1[i][:, t:t + 1], ALU.subtract, ALU.mult)
                ins.then_inc(c_ln[i][4], 1)

            def body1(b):
                for u in range(H):
                    if has(b, 0):
                        n = 16 * b + u
                        dve.wait_ge(c_s, n + 1)
                        ge(dve, c_mul, n - 1)
                        nc.vector.tensor_scalar(clip[:, u % 2, :], ps_a[u % 2][:, :], -CLAMP / SCALE1, CLAMP / SCALE1,
                                                ALU.max, ALU.min).then_inc(c_clip, 1)
                    h, off = at(u, 2)
                    if has(b, off):
                        n = 16 * (b + off) + h
                        dve.wait_ge(c_mul, n + 1)
                        ge(dve, c_exp, n - 3)
                        nc.vector.tensor_reduce(negmax1[:, h % 4, :], dec[:, h % 4, :].rearrange("p (t k) -> p t k", t=NT),
                                                AX.X, ALU.max, negate=True).then_inc(c_max, 1)
                    if u == 0 and has(b, 1):
                        ge(dve, c_ln[0][4], b + 1)
                        ln_stats1(0, b + 1)
                    if u == 1 and has(b, 1):
                        ge(dve, c_xt, b + 1)
                        normalise1(0, b + 1, xn3)
                    if u == 5 and has(b, -1):
                        dve.wait_ge(c_ok, 2 * b)
                        ge(dve, c_o, b - 1)
                        nc.vector.reciprocal(rs1[:, :, :, :, :].rearrange("p a w t j -> p (a w t j)"),
                                             ok1[:, :, :, :, :, HS].rearrange("p a w t j -> p (a w t j)")
                                             ).then_inc(c_rc, 1)
                    if u == 6 and has(b, 1):
                        dve.wait_ge(c_khi, b + 2)
                        for lo, hi, part in ((0, 2, 0), (3, 1, 1)):
                            ins = nc.vector.tensor_tensor(hl1[:, lo, :], ps_m[1][:, part * T:(part + 1) * T],
                                                          hl1[:, hi, :].bitcast(F32), ALU.subtract)
                        ins.then_inc(c_lo, 1)
                    if u == 9 and has(b, -1):
                        dve.wait_ge(c_y, b)
                        ge(dve, c_x, b - 1)
                        nc.vector.tensor_tensor(yg[:, :, :], ps_m[1][:, 0:T].rearrange("p (t c) -> p t c", t=NT),
                                                tabs[:, ds(b - 1), 4, :].broadcast_to([128, NT, C]),
                                                ALU.mult).then_inc(c_yg, 1)
                    if u == 11 and has(b, -1):
                        dve.wait_ge(c_x, b)
                        ge(dve, c_ln[1][4], b - 1)
                        ln_stats1(1, b - 1)
                    if u == 12 and has(b, -1):
                        ge(dve, c_h4p, b - 1)
                        normalise1(1, b - 1, xn4)

            dve.wait_ge(s_zx, B)
            run_loop(dve, body1)

            steps[0] = 0

            def step1(ins):
                steps[0] += 1
                ins.then_inc(f_r, 1)
                dve.wait_ge(f_r, steps[0])

            over1 = lambda t: t[:, :].unsqueeze(2).broadcast_to([128, B * NT, E1])
            iota1 = wl("iota", 0, E1).unsqueeze(1).broadcast_to([128, B * NT, E1])
            dve.wait_ge(f_lg, 1)
            logits = ps_a[0][:, 0:B * NT * E1].rearrange("p (a e) -> p a e", e=E1)
            step1(nc.vector.tensor_reduce(cols1[0][:, :], logits, AX.X, ALU.max))
            step1(nc.vector.tensor_tensor(lg1[:, :, :], logits, over1(cols1[0]), ALU.subtract))
            dve.wait_ge(f_exp, 1)
            step1(nc.vector.tensor_reduce(cols1[0][:, :], lg1[:, :, :], AX.X, ALU.add))
            step1(nc.vector.reciprocal(cols1[0][:, :], cols1[0][:, :]))
            step1(nc.vector.tensor_tensor(lg1[:, :, :], lg1[:, :, :], over1(cols1[0]), ALU.mult))
            for k in range(2):
                src = [lg1, sc1][k]
                step1(nc.vector.tensor_reduce(cols1[0][:, :], src[:, :, :], AX.X, ALU.max))
                step1(nc.vector.tensor_tensor(eq1[:, :, :], src[:, :, :], over1(cols1[0]), ALU.is_equal))
                step1(nc.vector.scalar_tensor_tensor(key1[:, :, :], eq1[:, :, :], -64.0, iota1, ALU.mult, ALU.add))
                step1(nc.vector.tensor_reduce(cols1[1][:, :], key1[:, :, :], AX.X, ALU.min))
                step1(nc.vector.tensor_tensor([pick1, eq1][k][:, :, :], key1[:, :, :], over1(cols1[1]), ALU.is_equal))
                if k == 0:
                    step1(nc.vector.scalar_tensor_tensor(flat2(sc1), flat2(pick1), -4.0, flat2(lg1), ALU.mult, ALU.add))
            step1(nc.vector.tensor_tensor(flat2(pick1), flat2(pick1), flat2(eq1), ALU.add))
            step1(nc.vector.tensor_tensor(w9[:, :, 0:E1], pick1[:, :, :], lg1[:, :, :], ALU.mult))
            step1(nc.vector.memset(w9[:, :, E1:E1 + 1], 1.0))
            assert steps[0] == W9_STEPS, steps[0]

            nc.vector.memset(acc[:, :, :, :], 0.0).then_inc(f_acc, ACC_STEPS * NT)
            dve.wait_ge(f_acc, ACC_STEPS * NT)

            def token_tile(c, i, t):
                base = ACC_STEPS * (NT * (c + 1) + t)
                k = [0]
                w = lambda e: w9[:, ds(NT * c + t), e]
                tile = lambda a: a.unsqueeze(1)

                def link1(ins):
                    k[0] += 1
                    ins.then_inc(f_acc, 1)

                def then():
                    dve.wait_ge(f_acc, base + k[0])

                dve.wait_ge(f_se, NT * c + t + 1)
                expert = lambda e: [[ps_a[0], ps_a[1]], [ps_m[0], ps_m[1]]][t][e // 4][:, e % 4 * C:(e % 4 + 1) * C]
                link1(nc.vector.tensor_scalar(acc[:, t, 0, :], expert(0), w(0), None, ALU.mult))
                for e in range(1, E1):
                    then()
                    link1(nc.vector.scalar_tensor_tensor(acc[:, t, e % 2, :], expert(e), w(e), acc[:, t, 1 - e % 2, :],
                                                         ALU.mult, ALU.add))
                then()
                link1(nc.vector.tensor_tensor(acc[:, t, 0, :], acc[:, t, 1, :], ps_pv[t][:, 0:C], ALU.add))
                then()
                link1(nc.vector.tensor_tensor(tile(acc[:, t, 1, :]), tile(acc[:, t, 0, :]), tabs[:, ds(c), 5, :], ALU.mult))
                then()
                link1(nc.vector.tensor_tensor(x_all[:, ds(NT * c + t), :], tile(acc[:, t, 1, :]), x_all[:, ds(NT * c + t), :],
                                              ALU.add))
                assert k[0] == ACC_STEPS

            with dve.Fori(0, B // 2) as pair:
                for i in range(2):
                    for t in range(NT):
                        token_tile(2 * pair + i, i, t)

        @block.tensor
        def _(pe):
            mm = nc.tensor.matmul
            pe.wait_ge(s_in, 16)
            pe.wait_ge(s_set, 3)
            for l in range(2):
                for i, chunk in enumerate((0, 1, 3, 4)):
                    k = 4 * l + i
                    ins = mm(ps_m[0][:, k * B:(k + 1) * B], we(f"wmod{l}", chunk * C, C), silu[:, l * B:(l + 1) * B],
                             start=True, stop=True)
            ins.then_inc(s_setp, 1)
            for l in range(2):
                for i, chunk in enumerate((2, 5)):
                    k = 2 * l + i
                    ins = mm(ps_m[1][0:8, k * C:(k + 1) * C], silu[:, l * B:(l + 1) * B], we(f"wmod{l}", chunk * C, C),
                             start=True, stop=True)
            ins.then_inc(s_setp, 1)
            pe.wait_ge(s_rows, 16)
            pe.wait_ge(s_const, 4)
            mm(ps_a[0][0:8, :], ones[0:1, 0:8], wr("gammas"), start=True, stop=True).then_inc(s_setp, 1)
            pe.wait_ge(s_set, 5)
            mm(ps_m[0][:, 0:1], ones[0:1, 0:128], wr("lamb"), start=True, stop=True).then_inc(s_setp, 1)
            pe.wait_ge(s_set, 20)
            for i in range(4):
                if i:
                    pe.wait_ge(s_seta, 1 + i)
                for k in range(2):
                    for n, (lo, hi) in enumerate(((0, 4), (4, 6))):
                        ins = mm([ps_a, ps_b][k][n][:, 0:(hi - lo) * C],
                                 ident[0:8, 2 * i + k:2 * i + k + 1].broadcast_to([8, 128]),
                                 tab8[:, lo:hi, :].rearrange("p a c -> p (a c)"), start=True, stop=True)
                ins.then_inc(s_setp, 1)
            pe.wait_ge(s_seta, 5)

            def a_fill(b, u, j):
                n, g, w = 32 * b + 4 * u + j, u // 2, u % 2
                if w == 0 and j == 0:
                    pe.wait_ge(s_st[g], 64 * (b + 1) + 16)
                ge(pe, s_a_max, n - 1)
                rows_j = slice(32 * j, 32 * j + 32)
                for t in range(NT):
                    ins = mm(ps_a[j % 2][:, t * T:(t + 1) * T], stack[rows_j, g, 0, w, t * 128:(t + 1) * 128],
                             stack[rows_j, g, 1, w, :], start=True, stop=True)
                ins.then_inc(s_a_full, 1)

            def b_fill(b, r, j):
                n, g, w = 32 * b + 4 * r + j, r // 2, r % 2
                if w == 0 and j == 0:
                    pe.wait_ge(s_mrow[g], 16 * (b + 1))
                ge(pe, s_exp, n - 1)
                rows_j = slice(32 * j, 32 * j + 32)
                for t in range(NT):
                    ins = mm(ps_b[j % 2][:, t * T:(t + 1) * T], stack[rows_j, g, 1, w, t * 128:(t + 1) * 128],
                             stack[rows_j, g, 0, w, :], start=True, stop=True)
                ins.then_inc(s_b_full, 1)

            def pv(b, r):
                g, w = r // 2, r % 2
                pe.wait_ge(s_exp, 32 * b + 4 * r + 4)
                pe.wait_ge(s_vc, 2 * b + 1 + g // 2)
                if w == 0:
                    ge(pe, s_ot, 4 * b + g - 1)
                for t in range(NT):
                    for j in range(J):
                        ins = mm(ps_pv[g % 2][32 * j:32 * j + 32, w * T:(w + 1) * T], v32[:, t, J * g + j, :],
                                 probs[:, r % 2, j, t * T:(t + 1) * T], start=(t == 0), stop=(t == NT - 1))
                ins.then_inc(s_pv, 1)

            def turn_max(b, g, it):
                wait_emptied(pe, 0, f"mT{g}", it)
                pe.wait_ge(s_mlo, 4 * b + g + 1)
                for x_ in range(2 * NT):
                    ins = nc.tensor.transpose(ps_m[0][0:8, x_ * 128:(x_ + 1) * 128],
                                              mhl[:, g, x_, :, :].rearrange("p j s -> p (j s)").bitcast(F32), ident)
                ins.then_inc(s_mtr, 1)

            def turn_pv(b, g, it):
                wait_emptied(pe, 1, f"oT{g}", it)
                pe.wait_ge(s_ot, 4 * b + g + 1)
                for x_ in range(2 * NT):
                    ins = nc.tensor.transpose(ps_m[1][:, x_ * 128:(x_ + 1) * 128],
                                              ot[:, g % 2, x_ * 128:(x_ + 1) * 128], ident)
                ins.then_inc(s_otr, 1)

            def turn(bank, src, s):
                for t in range(NT):
                    ins = nc.tensor.transpose(ps_m[bank][:, t * 128:(t + 1) * 128], src[:, t, :], ident)
                ins.then_inc(s, 1)

            def project(bank, first, s):
                for w in range(2):
                    ins = mm(ps_m[bank][:, w * T:(w + 1) * T], we("wqk0", (first + w) * C, C), ht[:, :],
                             start=True, stop=True)
                ins.then_inc(s, 1)

            def body(b):
                for u in range(8):
                    bb, off, r = b_round(b, u)
                    pb, poff, pr = pv_round(b, u)
                    for j in range(4):
                        if j == 2:
                            if has(b, poff):
                                pv(pb, pr)
                            if u == 0 and has(b, -1):
                                turn_max(b - 1, 3, b)
                            if u in (2, 4, 6) and has(b, 0):
                                turn_max(b, u // 2 - 1, b)
                        if has(b, 0):
                            a_fill(b, u, j)
                        if has(b, off):
                            b_fill(bb, r, j)
                    if pr % 2 and has(b, poff):
                        turn_pv(pb, pr // 2, b)
                    if u == 2 and has(b, 1):
                        wait_emptied(pe, 0, "xT", b)
                        pe.wait_ge(s_ln[0][4], b + 2)
                        turn(0, xn1, s_xt)
                    if u == 5 and has(b, 1):
                        pe.wait_ge(s_ht, b + 2)
                        wait_emptied(pe, 0, "q", b)
                        project(0, 0, s_q)
                        wait_emptied(pe, 1, "k", b)
                        project(1, 2, s_k)
                    if u == 6 and has(b, 1):
                        wait_emptied(pe, 0, "v", b)
                        for t in range(NT):
                            ins = mm(ps_m[0][:, t * C:(t + 1) * C], ht[:, t * 128:(t + 1) * 128], we("wv0"),
                                     start=True, stop=True)
                        ins.then_inc(s_v, 1)
                    if u == 7 and has(b, -1):
                        wait_emptied(pe, 1, "h2T", b)
                        pe.wait_ge(s_ln[2][4], b)
                        turn(1, xn2, s_h2p)

            run_loop(pe, body)

            pe.wait_ge(s_late, 16)
            pe.wait_ge(s_h2, B)
            pe.wait_ge(s_a_max, 32 * B)
            for t in range(B * NT):
                o = ps_a[0][:, t * E0:(t + 1) * E0]
                mm(o, ones[0:1, 0:128], wr("bg"), start=True, stop=False)
                ins = mm(o, h2t[:, t * 128:(t + 1) * 128], wl("wg"), start=False, stop=True)
            ins.then_inc(s_lg, 1)
            pe.wait_ge(s_exp, 32 * B)

            def hidden(n):
                f, c = n % NF0, n // NF0
                ge(pe, s_ge, n - 1)
                mm(ps_b[n % 2][:, :], wl("w1", f * 128, 128), h2t[:, c * 512:(c + 1) * 512], start=True,
                   stop=True).then_inc(s_g, 1)

            for n in range(10):
                hidden(n)
            pe.wait_ge(s_r, 23)
            for t in range(NT):
                ins = nc.tensor.transpose(ps_a[1][:, t * 128:(t + 1) * 128],
                                          rt[:, t, :, :].rearrange("p b e -> p (b e)"), ident)
            ins.then_inc(s_rt, 1)
            for n in range(10, 16):
                hidden(n)
            pe.wait_ge(s_ge, 16)
            pe.wait_ge(s_gs, 2)
            pe.wait_ge(s_r, 23 + 2 * (T // 16) + 2)
            pe.wait_ge(s_ot, 4 * B)
            with pe.Fori(0, B // 2) as pair:
                b = 2 * pair
                for i in range(2):
                    for f in range(NF0):
                        ins = mm([ps_a, ps_b][i][f // 2][:, f % 2 * T:(f % 2 + 1) * T],
                                 spread[:, ds((E0 * (b + i) + 4 * f) * F0, 128)], selb[:, :], start=True, stop=True)
                    ins.then_inc(s_mask, 1)
                for i in range(2):
                    pe.wait_ge(s_hm, b + i + 1)
                    pe.wait_ge(s_h2c, b + i + 1)
                    for t in range(NT):
                        o = ps_pv[i][:, t * C:(t + 1) * C]
                        for f in range(NF0):
                            mm(o, hm[:, i, f, t * 128:(t + 1) * 128], wl("w2", f * C, C), start=(f == 0), stop=False)
                        mm(o, sel[:, t * 128:(t + 1) * 128], b2m[:, ds(b + i), :].rearrange("p a c -> p (a c)"),
                           start=False, stop=False)
                        ins = mm(o, h2c[:, i, t * 128:(t + 1) * 128], ident, start=False, stop=True)
                    ins.then_inc(s_z, 1)
                for i in range(2):
                    pe.wait_ge(s_zn, b + i + 1)

            pe.wait_ge(s_hm, B)
            pe.wait_ge(s_small, 32)
            pe.wait_ge(c_w, 1)
            mm(ps_a[0][0:32, 0:C], wl("wdown"), wkv[:, :], start=True, stop=True).then_inc(c_wp, 1)
            pe.wait_ge(c_w, 2)
            mm(ps_a[1][:, 0:2 * C], wlat[:, :], wup_s[:, :], start=True, stop=True).then_inc(c_wp, 1)
            pe.wait_ge(c_w, 3)

            def scores1(b, h):
                n, g, j = 16 * b + h, h // 4, h % 4
                if j == 0:
                    pe.wait_ge(c_st[g], 64 * (b + 1))
                ge(pe, c_clip, n - 1)
                rows_j = slice(32 * j, 32 * j + 32)
                for t in range(NT):
                    ins = mm(ps_a[h % 2][:, t * T:(t + 1) * T], stack1[rows_j, g, 0, t * 128:(t + 1) * 128],
                             stack1[rows_j, g, 1, :], start=True, stop=True)
                ins.then_inc(c_s, 1)

            def turn_exp(b, h):
                n = 16 * b + h
                pe.wait_ge(c_exp, n + 1)
                ge(pe, c_ev, n - 1)
                for k in range(NT):
                    for t in range(NT):
                        ins = nc.tensor.transpose(ps_b[h % 2][:, k * T + t * 128:k * T + (t + 1) * 128],
                                                  prob1[:, h % 2, t * T + k * 128:t * T + (k + 1) * 128], ident)
                ins.then_inc(c_pt, 1)

            def pv1(b, r):
                pe.wait_ge(c_ev, 16 * b + 4 * r + 4)
                pe.wait_ge(c_vc, 2 * b + 1 + r // 2)
                if r % 2 == 0:
                    ge(pe, c_ot, 2 * b + r // 2 - 1)
                for k in range(NT):
                    for j in range(J):
                        ins = mm(ps_pv[r // 2][32 * j:32 * j + 32, r % 2 * T:(r % 2 + 1) * T], v32[:, k, J * r + j, :],
                                 probt[:, r % 2, j, k * T:(k + 1) * T], start=(k == 0), stop=(k == NT - 1))
                ins.then_inc(c_pv, 1)

            def body1(b):
                for u in range(H):
                    if has(b, 0):
                        scores1(b, u)
                    h, off = at(u, 4)
                    if has(b, off):
                        turn_exp(b + off, h)
                    for r, tick, off in ((0, 8, 0), (1, 12, 0), (2, 0, -1), (3, 4, -1)):
                        if u == tick and has(b, off):
                            pv1(b + off, r)
                    for p, tick, off in ((0, 13, 0), (1, 5, -1)):
                        if u == tick and has(b, off):
                            wait_emptied(pe, 1, f"t{p}", b, ORDER_1)
                            pe.wait_ge(c_ot, 2 * (b + off) + p + 1)
                            for k in range(2 * NT):
                                ins = nc.tensor.transpose(ps_m[1][:, k * 128:(k + 1) * 128],
                                                          ot1[:, p, k * 128:(k + 1) * 128], ident)
                            ins.then_inc(c_otr, 1)
                    if u == 3 and has(b, 1):
                        wait_emptied(pe, 0, "xT", b, ORDER_1)
                        pe.wait_ge(c_ln[0][4], b + 2)
                        turn(0, xn3, c_xt)
                    if u == 6 and has(b, 1):
                        wait_emptied(pe, 1, "qk", b, ORDER_1)
                        pe.wait_ge(c_ht, b + 2)
                        mm(ps_m[1][:, 0:T], wl("wq"), ht1[:, :], start=True, stop=True)
                        mm(ps_m[1][:, T:2 * T], wrec[:, 0:C], ht1[:, :], start=True, stop=True).then_inc(c_qk, 1)
                    if u == 7 and has(b, 1):
                        wait_emptied(pe, 0, "v", b, ORDER_1)
                        for t in range(NT):
                            ins = mm(ps_m[0][:, t * C:(t + 1) * C], ht1[:, t * 128:(t + 1) * 128], wrec[:, C:2 * C],
                                     start=True, stop=True)
                        ins.then_inc(c_v, 1)
                    if u == 8 and has(b, -1):
                        wait_emptied(pe, 0, "oT", b, ORDER_1)
                        pe.wait_ge(c_o, b)
                        turn(0, o1, c_oT)
                    if u == 9 and has(b, -1):
                        wait_emptied(pe, 1, "y", b, ORDER_1)
                        pe.wait_ge(c_ots, b)
                        for t in range(NT):
                            ins = mm(ps_m[1][:, t * C:(t + 1) * C], o1t[:, t * 128:(t + 1) * 128], wl("wo"),
                                     start=True, stop=True)
                        ins.then_inc(c_y, 1)
                    if u == 14 and has(b, -1):
                        wait_emptied(pe, 0, "h4T", b, ORDER_1)
                        pe.wait_ge(c_ln[1][4], b)
                        turn(0, xn4, c_h4p)

            run_loop(pe, body1)

            pe.wait_ge(c_h4, B)
            pe.wait_ge(c_clip, 16 * B)
            for t in range(B * NT):
                o = ps_a[0][:, t * E1:(t + 1) * E1]
                mm(o, ones[0:1, 0:128], wr("rb"), start=True, stop=False)
                ins = mm(o, h2t[:, t * 128:(t + 1) * 128], wl("router"), start=False, stop=True)
            ins.then_inc(f_lg, 1)
            pe.wait_ge(f_r, W9_STEPS)
            pe.wait_ge(c_ot, 2 * B)
            for i in range(4):
                if i >= 2:
                    pe.wait_ge(f_wtc, i - 1)
                for k in range(4):
                    ins = nc.tensor.transpose(ps_pv[i % 2][0:E1 + 1, k * 128:(k + 1) * 128], w9[:, 4 * i + k, :], ident)
                ins.then_inc(f_wt, 1)

            pe.wait_ge(c_ev, 16 * B)
            pe.wait_ge(f_wtc, 4)

            def hidden1(c, i, f2):
                ge(pe, f_ge, 9 * c + f2 - 1)
                for k in range(2):
                    ins = mm(ps_b[(i + f2) % 2][:, k * T:(k + 1) * T], wl("w1b", (2 * f2 + k) * 128, 128),
                             h2t[:, ds(T * c, T)], start=True, stop=True)
                ins.then_inc(f_h, 1)

            def second(c, i, t):
                pe.wait_ge(f_ge, 9 * c + 9)
                pe.wait_ge(f_wc, c + 1)
                pe.wait_ge(f_acc, ACC_STEPS * (NT * c + t + 1))
                shared = ps_pv[t][:, 0:C]
                mm(shared, w9c[:, i, t * 128:(t + 1) * 128], rb2_s[:, :], start=True, stop=False)
                for f in range(NF1):
                    lhs = hid[:, i, f, t * 128:(t + 1) * 128]
                    e = (f - 2) // 2
                    o = shared if f < 2 else [ps_a, ps_m][t][e // 4][:, e % 4 * C:(e % 4 + 1) * C]
                    ins = mm(o, lhs, wl("w2b", f * C, C), start=(f % 2 == 0 and f >= 2), stop=(f % 2 == 1))
                ins.then_inc(f_se, 1)

            for f2 in range(NF1 // 2):
                hidden1(0, 0, f2)

            def chunk(c, i, last=False):
                for f2 in range(NF1 // 2):
                    if not last:
                        hidden1(c + 1, 1 - i, f2)
                    if f2 in (1, 5):
                        second(c, i, f2 // 4)

            with pe.Fori(0, B // 2 - 1) as pair:
                for i in range(2):
                    chunk(2 * pair + i, i)
            chunk(B - 2, 0)
            chunk(B - 1, 1, last=True)


def layout(i):
    import numpy as np
    f = {k: np.asarray(v) for k, v in i.items()}
    heads = lambda w: w.transpose(1, 0, 2).reshape(C, H * HS)
    tiles = lambda w, n: w.reshape(n, 128, -1).transpose(1, 0, 2).reshape(128, -1)
    p = np.arange(128)
    eye = np.eye(128, dtype=np.float32)
    at = np.arange(T, dtype=np.float32)
    decay = np.exp(np.float32(-0.01 * 0.01) * np.abs(at[:, None] - at[None, :])) * np.float32(SCALE1)
    e = {"ct": np.concatenate([f["L0_c"].T, f["L1_c"].T], 1), "wmod0": f["L0_wmod"], "wmod1": f["L1_wmod"],
         "wqk0": np.concatenate([heads(f[f"L0_attn_{n}"]) for n in ("wq1", "wq2", "wk1", "wk2")], 1),
         "wv0": heads(f["L0_attn_wv"]), "ident": eye}
    l = {"wg": f["L0_ffn_wg"], "w1": f["L0_ffn_w1"].transpose(1, 0, 2).reshape(C, E0 * F0),
         "b1": f["L0_ffn_b1"].reshape(NF0, 128).T, "w2": tiles(f["L0_ffn_w2"].reshape(E0 * F0, C), NF0),
         "iota": np.broadcast_to(np.arange(E0, dtype=np.float32), (128, E0)),
         "blocks": (p[:, None] // E0 == np.arange(B)[None, :]).astype(np.float32),
         "wq": f["L1_attn_Wq"], "wkt": f["L1_attn_Wk"].T, "wvt": f["L1_attn_Wv"].T, "wo": f["L1_attn_Wo"],
         "wdown": f["L1_attn_W_down_kv"], "router": f["L1_ffn_router_w"],
         "w1b": np.concatenate([f["L1_ffn_sw1"], f["L1_ffn_rw1"].transpose(1, 0, 2).reshape(C, E1 * F1)], 1),
         "b1b": np.concatenate([f["L1_ffn_sb1"], f["L1_ffn_rb1"].reshape(-1)]).reshape(NF1, 128).T,
         "w2b": np.concatenate([tiles(f["L1_ffn_sw2"], 2), tiles(f["L1_ffn_rw2"].reshape(E1 * F1, C), NF1 - 2)], 1),
         "decay": tiles(decay, NT)}
    r = {"gammas": np.concatenate([f[f"L0_{n}"] for n in ("attn_ln_gamma", "attn_ln_beta", "ffn_gamma", "ffn_beta")]),
         "lamb": f["L0_attn_lamb"].reshape(1), "bg": f["L0_ffn_bg"], "rb": f["L1_ffn_router_b"]}
    pack = lambda parts, d: np.ascontiguousarray(np.concatenate([d[n].reshape(-1, k) for n, k in parts], 1))
    return {"x": np.ascontiguousarray(f["L0_attn_x"].reshape(B * NT, 128, C).transpose(1, 0, 2)),
            "early": pack(EARLY, e), "late": pack(LATE, l), "rows": pack(ROWS, r), "b2": f["L0_ffn_b2"],
            "wup": np.concatenate([f["L1_attn_W_up_k"], f["L1_attn_W_up_v"]], 1),
            "rb2": np.concatenate([f["L1_ffn_rb2"], f["L1_ffn_sb2"][None]], 0)}


def kernel(**inputs):
    import numpy as np
    import concourse.bacc as bacc
    from concourse.bass_utils import run_bass_kernel_spmd
    nc = bacc.Bacc("TRN2", target_bir_lowering=False, num_devices=1)
    arrays, args = {}, {}
    for name, a in layout(inputs).items():
        arrays[f"in_{name}"] = a
        args[name] = nc.dram_tensor(f"in_{name}", a.shape, mybir.dt.from_np(a.dtype), kind="ExternalInput").ap()
    out = nc.dram_tensor("out", (128, B * NT, C), F32, kind="ExternalOutput").ap()
    build(nc, **args, out=out)
    got = run_bass_kernel_spmd(nc, [arrays], core_ids=[0]).results[0]["out"]
    return np.ascontiguousarray(got.transpose(1, 0, 2)).reshape(B, T, C)
```

```python
import concourse.bass as bass
from concourse import mybir
from contextlib import ExitStack

F32 = mybir.dt.float32
F32R = mybir.dt.float32r
BF16 = mybir.dt.bfloat16
ALU = mybir.AluOpType
ACT = mybir.ActivationFunctionType
AX = mybir.AxisListType

B, T, C, H, HS = 8, 256, 128, 16, 8
NT = T // 128
G, J = 4, 4
E0, F0 = 16, 32
E1, F1 = 8, 256
NF0 = E0 * F0 // 128
NF1 = F1 // 128 + E1 * F1 // 128
EPS = 1e-5
CLAMP = 10000.0
SCALE0 = float(HS) ** -0.5
SCALE1 = 1.0 / (float(C) ** 0.5 + 1e-8)
ACC_STEPS = E1 + 3
W9_STEPS = 19
EARLY_HIDDEN = 6

EARLY = [("ct", 2 * B), ("wmod0", 6 * C), ("wmod1", 6 * C), ("wqk0", 4 * C), ("wv0", C), ("ident", 128)]
LATE = [("wg", E0), ("w1", E0 * F0), ("b1", NF0), ("w2", NF0 * C), ("iota", E0), ("blocks", B),
        ("wq", C), ("wkt", C), ("wvt", C), ("wo", C), ("wdown", 32), ("router", E1),
        ("w1b", NF1 * 128), ("b1b", NF1), ("w2b", NF1 * C), ("decay", NT * T)]
ROWS = [("gammas", 4 * C), ("lamb", 1), ("bg", E0), ("rb", E1)]


def spans(parts):
    at, out = 0, {}
    for name, n in parts:
        out[name] = (at, at + n)
        at += n
    return out, at


EARLY_AT, N_EARLY = spans(EARLY)
LATE_AT, N_LATE = spans(LATE)
ROWS_AT, N_ROWS = spans(ROWS)


def ds(i, n=1):
    return bass.ds(i, n)


def build(nc, x, early, late, rows, b2, wup, rb2, out):
    ctx = ExitStack()
    with ctx:
        scope = [ctx]

        def sb(name, shape, dt=F32):
            return scope[0].enter_context(nc.sbuf_tensor(name, shape, dt))

        def new_scope():
            if scope[0] is not ctx:
                scope[0].close()
            scope[0] = ctx.enter_context(ExitStack())

        def sem(name):
            return ctx.enter_context(nc.semaphore(name))

        banks = [ctx.enter_context(nc.psum_tensor(f"bank{i}", [128, 512], F32)) for i in range(8)]
        ps_a, ps_b, ps_pv, ps_m = banks[0:2], banks[2:4], banks[4:6], banks[6:8]

        w_early = sb("w_early", [128, N_EARLY])
        w_late = sb("w_late", [128, N_LATE])
        w_rows = sb("w_rows", [1, N_ROWS])

        def we(name, a=0, n=None):
            lo, hi = EARLY_AT[name]
            return w_early[:, lo + a:hi if n is None else lo + a + n]

        def wl(name, a=0, n=None):
            lo, hi = LATE_AT[name]
            return w_late[:, lo + a:hi if n is None else lo + a + n]

        def wr(name):
            lo, hi = ROWS_AT[name]
            return w_rows[0:1, lo:hi]

        ident = we("ident")
        ones = sb("ones", [128, 512])
        zeros = sb("zeros", [8, 512])
        x_all = sb("x_all", [128, B * NT, C])
        h2t = sb("h2t", [128, B * T])
        silu = sb("silu", [128, 2 * B])
        silu_t = sb("silu_t", [128, 2 * B])
        mod_c = sb("mod_c", [128, 8, B])
        tab8 = sb("tab8", [8, 6, C])
        gate8 = sb("gate8", [8, 4, C])
        gpos = sb("gpos", [8, 4, C])
        gmax = sb("gmax", [8, 4, C])
        gam8 = sb("gam8", [8, 4, C])
        lam_c = sb("lam_c", [128, 2])
        tabs = sb("tabs", [128, B, 6, C])

        s_in = sem("early_loaded")
        s_xin = sem("x_loaded")
        s_late = sem("late_loaded")
        s_rows = sem("rows_loaded")
        s_const = sem("constants_set")
        s_set = sem("setup_vector")
        s_seta = sem("setup_scalar")
        s_setp = sem("setup_tensor")
        s_rows_d = sem("table_rows_in_dram")
        s_tabs = sem("tables_spread")
        rows_d = nc.dram_tensor("table_rows", (B, 6 * C), F32, kind="Internal").ap()
        s_setg = sem("setup_gpsimd")

        spread = sb("spread", [128, 128 * F0], BF16)
        b2t = sb("b2t", [128, C])
        b2m = sb("b2m", [128, B, C])
        half = sb("half", [128, NT])
        eps_c = sb("eps_c", [128, NT])
        spare = sb("spare", [128, 64])

        vs = sb("vs", [128, NT, H, HS])
        v32 = sb("v32", [128, NT, H, 32])
        wup_s = sb("wup_s", [32, 2 * C])
        rb2_s = sb("rb2_s", [E1 + 1, C])
        wkv = sb("wkv", [128, C])
        wlat = sb("wlat", [32, C])
        wrec = sb("wrec", [128, 2 * C])
        s_small = sem("small_loaded")
        stack1 = sb("stack1", [128, G, 2, T], F32R)
        stats1 = [sb(f"stats1_{i}", [128, NT, 6]) for i in range(2)]
        meanvar1 = [sb(f"meanvar1_{i}", [128, NT, 2]) for i in range(2)]
        rstd1 = [sb(f"rstd1_{i}", [128, NT]) for i in range(2)]
        xn3 = sb("xn3", [128, NT, C])
        ht1 = sb("ht1", [128, T])
        hl1 = sb("hl1", [128, 4, T], F32R)

        new_scope()
        stack = sb("stack", [128, G, 2, 2, T], F32R)
        probs = sb("probs", [128, 2, J, NT * T])
        stats = [sb(f"stats{i}", [128, NT, 6]) for i in range(3)]
        meanvar = [sb(f"meanvar{i}", [128, NT, 2]) for i in range(3)]
        rstd = [sb(f"rstd{i}", [128, NT]) for i in range(3)]
        xn1 = sb("xn1", [128, NT, C])
        ht = sb("ht", [128, T])
        hl = sb("hl", [128, 4, 2, T], F32R)
        negmax = sb("negmax", [128, G, 2, NT, J])
        mhl = sb("mhl", [128, G, 2 * NT, J, 2], F32R)
        mrow = sb("mrow", [8, G, 512], F32R)
        ot = sb("ot", [128, 2, 2 * T])
        ok = sb("ok", [128, G, 2, NT, J, HS + 1])
        rs = sb("rs", [128, G, 2, NT * J])
        prod = sb("prod", [128, G, 2, NT, J * HS])
        o_t = sb("o_t", [128, NT, C])
        on = sb("on", [128, NT, C])
        og = sb("og", [128, NT, C])
        ob = sb("ob", [128, NT, C])
        xn2 = sb("xn2", [128, NT, C])

        s_a_full = sem("a_scores_done")
        s_a_max = sem("a_max_taken")
        s_b_full = sem("b_scores_done")
        s_exp = sem("exp_done")
        s_pv = sem("pv_done")
        s_ot = sem("pv_copied")
        s_otr = sem("pv_turned")
        s_ok = sem("pv_turned_copied")
        s_mhi = sem("max_high")
        s_mlo = sem("max_low")
        s_mtr = sem("max_turned")
        s_mcp = sem("max_turned_copied")
        s_st = [sem(f"stack_loaded{g}") for g in range(G)]
        s_mrow = [sem(f"max_rows_loaded{g}") for g in range(G)]
        s_ln = [[sem(f"ln{i}_{n}") for n in ("stats", "meanvar", "eps", "rstd", "normal")] for i in range(3)]
        s_xt = sem("x_turned")
        s_ht = sem("h_ready")
        s_q = sem("q_projected")
        s_k = sem("k_projected")
        s_v = sem("v_projected")
        s_qhi, s_khi, s_qlo, s_klo = sem("q_high"), sem("k_high"), sem("q_low"), sem("k_low")
        s_vs = sem("v_staged")
        s_vc = sem("v_spread")
        s_rc = sem("rowsum_inverse")
        s_pr = sem("o_scaled")
        s_o = sem("o_ready")
        s_og, s_ob, s_xc = sem("o_gamma"), sem("o_beta"), sem("x_new")
        s_h2p = sem("h2_turned")
        s_h2 = sem("h2_ready")

        new_scope()
        h1 = sb("h1", [128, NF0, B * T])
        lg = sb("lg", [128, B * NT, E0])
        sc = sb("sc", [128, B * NT, E0])
        key = sb("key", [128, B * NT, E0])
        eq = sb("eq", [128, B * NT, E0])
        pick = sb("pick", [128, B * NT, E0])
        col = [sb(f"col{i}", [128, B * NT]) for i in range(2)]
        rt = sb("rt", [128, NT, B, E0])
        den = sb("den", [128, NT * E0])
        route = sb("route", [128, T])
        top8 = sb("top8", [128, 8])
        sel = sb("sel", [128, T])
        selb = sb("selb", [128, T], BF16)
        hm = sb("hm", [128, 2, NF0, T])
        h2c = sb("h2c", [128, 2, T])
        zn = sb("zn", [128, 2, NT, C])
        zg = sb("zg", [128, 2, NT, C])
        zb = sb("zb", [128, 2, NT, C])
        zst = sb("zst", [128, 2, NT, 6])
        zmv = sb("zmv", [128, 2, NT, 2])
        zrs = sb("zrs", [128, 2, NT])
        s_b2 = sem("b2_loaded")
        s_lg = sem("logits_done")
        s_r = sem("routing_vector")
        s_rexp = sem("routing_exp")
        s_rt = sem("route_turned")
        s_rtc = sem("route_turned_copied")
        s_g = sem("hidden_done")
        s_ge = sem("gelu_done")
        s_gs = sem("routing_gpsimd")
        s_mask = sem("mask_done")
        s_hm = sem("hidden_masked")
        s_z = sem("z_done")
        s_zst, s_zmv, s_zeps, s_zrs, s_zn = (sem(f"z_{n}") for n in ("stats", "meanvar", "eps", "rstd", "normal"))
        s_h2c = sem("h2_copied")
        s_zg, s_zb, s_zx = sem("z_gamma"), sem("z_beta"), sem("z_added")

        new_scope()
        clip = sb("clip", [128, 2, NT * T])
        dec = sb("dec", [128, 4, NT * T])
        prob1 = sb("prob1", [128, 2, NT * T])
        probt = sb("probt", [128, 2, J, NT * T])
        ot1 = sb("ot1", [128, 2, 2 * T])
        xn4 = sb("xn4", [128, NT, C])
        negmax1 = sb("negmax1", [128, 4, NT])
        ok1 = sb("ok1", [128, 2, 2, NT, J, HS + 1])
        rs1 = sb("rs1", [128, 2, 2, NT, J])
        o1 = sb("o1", [128, NT, C])
        o1t = sb("o1t", [128, T])
        yg = sb("yg", [128, NT, C])

        c_w = sem("weights_folded")
        c_wp = sem("weights_products")
        c_s, c_clip, c_mul, c_max = sem("scores1"), sem("clipped"), sem("decayed"), sem("max1")
        c_exp, c_pt, c_ev = sem("exp1"), sem("exp_turned"), sem("exp_turned_copied")
        c_pv = sem("pv1")
        c_ot, c_otr, c_ok = sem("pv1_copied"), sem("pv1_turned"), sem("pv1_turned_copied")
        c_ln = [[sem(f"ln1_{i}_{n}") for n in ("stats", "meanvar", "eps", "rstd", "normal")] for i in range(2)]
        c_xt, c_ht = sem("x1_turned"), sem("h1_ready")
        c_qk, c_qhi, c_khi, c_lo = sem("qk1"), sem("q1_high"), sem("k1_high"), sem("qk1_low")
        c_v, c_vs, c_vc = sem("v1"), sem("v1_staged"), sem("v1_spread")
        c_st = [sem(f"stack1_loaded{g}") for g in range(G)]
        c_rc, c_o, c_oT, c_ots = sem("inverse1"), sem("o1_ready"), sem("o1_turned"), sem("o1_turned_copied")
        c_y, c_yg, c_x = sem("y"), sem("y_gated"), sem("x3_ready")
        c_h4p, c_h4 = sem("h4_turned"), sem("h4_ready")

        new_scope()
        hid = sb("hid", [128, 2, NF1, T])
        lg1 = sb("lg1", [128, B * NT, E1])
        sc1 = sb("sc1", [128, B * NT, E1])
        key1 = sb("key1", [128, B * NT, E1])
        eq1 = sb("eq1", [128, B * NT, E1])
        pick1 = sb("pick1", [128, B * NT, E1])
        cols1 = [sb(f"cols1_{i}", [128, B * NT]) for i in range(2)]
        w9 = sb("w9", [128, B * NT, E1 + 1])
        w9t = sb("w9t", [E1 + 1, B * T])
        w9c = sb("w9c", [E1 + 1, 2, T])
        acc = sb("acc", [128, 2, 2, C])
        h4s = sb("h4s", [128, 2, 2, T], F32R)
        w1s = sb("w1s", [128, 2, NF1 * 128], F32R)
        f_w1h, f_w1l = sem("w1_high"), sem("w1_low")
        f_xh, f_xl = sem("input_high"), sem("input_low")
        f_lg, f_r, f_exp = sem("logits1"), sem("routing1_vector"), sem("routing1_exp")
        f_wt, f_wtc = sem("weights_turned"), sem("weights_turned_copied")
        f_h, f_ge = sem("hidden1"), sem("gelu1")
        f_wc = sem("weights_batch")
        f_se = sem("second_layer")
        f_acc = sem("sum_steps")
        f_out = sem("out_written")

        def at(u, lag):
            return (u - lag, 0) if u >= lag else (u - lag + H, -1)

        ORDER_1 = [
            [("xT", 1, c_ht, 1, 0), ("qk", 1, c_lo, 1, 0), ("h4T", -2, c_h4, 1, 0), ("v", 1, c_vs, 1, 0),
             ("oT", -1, c_ots, 1, 0)],
            [("t0", -1, c_ok, 2, 0), ("t1", -1, c_ok, 2, 1), ("y", -1, c_yg, 1, 0)]]

        ORDER_M = [
            [("mT3", -1, s_mcp, 4, 3), ("mT0", 0, s_mcp, 4, 0), ("xT", 1, s_ht, 1, 0), ("mT1", 0, s_mcp, 4, 1),
             ("q", 1, s_qlo, 1, 0), ("mT2", 0, s_mcp, 4, 2), ("v", 1, s_vs, 1, 0)],
            [("oT1", -1, s_ok, 4, 1), ("oT2", -1, s_ok, 4, 2), ("h2T", -2, s_h2, 1, 0), ("oT3", -1, s_ok, 4, 3),
             ("k", 1, s_klo, 1, 0), ("oT0", 0, s_ok, 4, 0)]]

        def wait_emptied(pe, bank, name, b, orders=ORDER_M):
            order = orders[bank]
            at = [u[0] for u in order].index(name)
            for back in range(1, 2 * len(order)):
                k, it = (at - back) % len(order), b + (at - back) // len(order)
                _, off, s, per, which = order[k]
                if isinstance(it, int) and not 0 <= it + off < B:
                    continue
                pe.wait_ge(s, per * (it + off) + which + 1)
                return

        def has(b, off):
            return not isinstance(b, int) or 0 <= b + off < B

        def run_loop(eng, body, aside=lambda: None, past=1, first=lambda: None, last=lambda: None,
                     started=False):
            if not started:
                body(-1)
            first()
            body(0)
            aside()
            for b in range(1, 1 + past):
                body(b)
            with eng.Fori(1 + past, B - 1) as b:
                body(b)
            for b in range(B - 1, B + past):
                if b == B + past - 1:
                    last()
                body(b)

        def over_pairs(eng, body, ahead):
            with eng.Fori(0, B // 2 - 2) as pair:
                for i in range(2):
                    body(2 * pair + i, i)
            for b in range(B - 4, B):
                ahead(-1, [range(0, 2), range(2, 4), range(4, 6), range(6, H)][b - (B - 4)])
                body(b, b % 2, last=(b == B - 1))

        def ge(eng, s, value, least=1):
            if not isinstance(value, int) or value >= least:
                eng.wait_ge(s, value)

        def b_round(b, u):
            return (b - 1, -1, u + 4) if u < 4 else (b, 0, u - 4)

        def pv_round(b, u):
            return (b - 1, -1, u + 3) if u < 5 else (b, 0, u - 5)

        held = [0]

        def hold(eng):
            k = held[0] = held[0] + 1
            if eng is nc.vector:
                eng.memset(spare[:, k:k + 1], 0.0)
            else:
                eng.tensor_tensor(spare[:, k:k + 1], half[:, 0:1], half[:, 0:1], ALU.mult)

        block = ctx.enter_context(nc.Block())

        @block.sync
        def _(sp):
            sp.dma_start(w_early[:, :], early).then_inc(s_in, 16)
            sp.dma_start(x_all[:, :, :], x).then_inc(s_xin, 16)
            sp.dma_start(w_rows[:, :], rows).then_inc(s_rows, 16)
            sp.dma_start(w_late[:, :], late).then_inc(s_late, 16)
            for b in range(B):
                sp.dma_start(b2t[E0 * b:E0 * b + E0, :], b2).then_inc(s_b2, 16)
            sp.dma_start(wup_s[:, :], wup).then_inc(s_small, 16)
            sp.dma_start(rb2_s[:, :], rb2).then_inc(s_small, 16)
            sp.wait_ge(s_const, 4)
            for g in range(G):
                sp.dma_start(stack[3::16, g, 1, :, :].bitcast(F32),
                             ones[0:8, :].rearrange("p (w t) -> p w t", w=2)).then_inc(s_st[g], 16)

            def load_stack(b, g):
                if g == 0:
                    sp.wait_ge(s_klo, b + 1)
                    sp.wait_ge(s_qlo, b + 1)
                ge(sp, s_b_full, 32 * b - 24 + 8 * g)
                rows_g = slice(32 * g, 32 * g + 32)
                for part, src in ((0, hl[rows_g, 2:0:-1]), (1, hl[rows_g, 2:4]), (2, hl[rows_g, 0:2])):
                    sp.dma_start(stack[part::4, g, :, :, :].bitcast(F32), src.bitcast(F32)).then_inc(s_st[g], 16)
                sp.dma_start(stack[3::16, g, 0, :, :].bitcast(F32),
                             zeros[:, :].rearrange("p (w t) -> p w t", w=2)).then_inc(s_st[g], 16)

            def load_max(b, g):
                sp.wait_ge(s_mcp, 4 * b + g + 1)
                sp.dma_start(stack[3::16, g, 0, :, :].bitcast(F32),
                             mrow[:, g, :].rearrange("p (w t) -> p w t", w=2).bitcast(F32)).then_inc(s_mrow[g], 16)

            def body(b):
                if has(b, -1):
                    load_max(b - 1, 3)
                if has(b, 0):
                    load_stack(b, 2)
                    load_max(b, 0)
                    load_stack(b, 3)
                    load_max(b, 1)
                if has(b, 1):
                    load_stack(b + 1, 0)
                if has(b, 0):
                    load_max(b, 2)
                if has(b, 1):
                    load_stack(b + 1, 1)

            run_loop(sp, body, past=2)

            def load_stack1(b, g):
                if g == 0:
                    sp.wait_ge(c_lo, b + 1)
                ge(sp, c_s, 16 * b - 12 + 4 * g)
                rows_g = slice(32 * g, 32 * g + 32)
                for part, src in ((0, hl1[rows_g, 2:0:-1]), (1, hl1[rows_g, 2:4]), (2, hl1[rows_g, 0:2]),
                                  (3, hl1[rows_g, 0:4:3])):
                    sp.dma_start(stack1[part::4, g, :, :].bitcast(F32), src.bitcast(F32)).then_inc(c_st[g], 16)

            def body1(b):
                if has(b, 0):
                    load_stack1(b, 3)
                if has(b, 1):
                    for g in range(3):
                        load_stack1(b + 1, g)

            run_loop(sp, body1, past=2)
            with sp.Fori(0, B) as b:
                sp.wait_ge(f_acc, ACC_STEPS * NT * (b + 2))
                sp.dma_start(out[:, ds(NT * b, NT), :], x_all[:, ds(NT * b, NT), :]).then_inc(f_out, 16)
            sp.wait_ge(f_out, 16 * B)

        @block.gpsimd
        def _(gp):
            gp.memset(zeros[:, :], 0.0).then_inc(s_const, 1)
            gp.memset(ones[:, :], 1.0).then_inc(s_const, 1)
            gp.memset(half[:, :], -0.5).then_inc(s_setg, 1)
            gp.memset(eps_c[:, :], EPS).then_inc(s_setg, 1)
            gp.memset(v32[:, :, :, :], 0.0).then_inc(s_setg, 1)
            gp.wait_ge(s_setg, 3)
            gp.memset(v32[:, :, :, HS:HS + 1], 1.0).then_inc(s_setg, 1)
            gp.wait_ge(s_setg, 4)

            def inverse_std(i, b):
                gp.wait_ge(s_ln[i][1], b + 1)
                gp.tensor_tensor(rstd[i][:, :], meanvar[i][:, :, 1], eps_c[:, :], ALU.add).then_inc(s_ln[i][2], 1)
                gp.wait_ge(s_ln[i][2], b + 1)
                gp.tensor_tensor(rstd[i][:, :], rstd[i][:, :], half[:, :], ALU.pow).then_inc(s_ln[i][3], 1)

            def normalise(i, b, dst, src):
                gp.wait_ge(s_ln[i][3], b + 1)
                hold(gp)
                for t in range(NT):
                    ins = gp.tensor_scalar(dst[:, t, :], src[:, t, :], meanvar[i][:, t, 0:1], rstd[i][:, t:t + 1],
                                           ALU.subtract, ALU.mult)
                ins.then_inc(s_ln[i][4], 1)

            def spread_v(b, part):
                gp.wait_ge(s_vs, b + 1)
                ge(gp, s_pv, 8 * b - 4 + 4 * part)
                hold(gp)
                hh = slice(8 * part, 8 * part + 8)
                gp.tensor_copy(v32[:, :, hh, 0:HS], vs[:, :, hh, :]).then_inc(s_vc, 1)

            def body(b):
                if has(b, 1):
                    inverse_std(0, b + 1)
                if has(b, 0):
                    spread_v(b, 0)
                if has(b, -2):
                    inverse_std(2, b - 2)
                if has(b, 0):
                    spread_v(b, 1)
                if has(b, -1):
                    c = b - 1
                    gp.wait_ge(s_rc, 2 * c + 2)
                    ge(gp, s_o, c)
                    gp.tensor_tensor(prod[:, :, :, :, :].rearrange("p g w t (j d) -> p (g w t j) d", d=HS),
                                     ok[:, :, :, :, :, 0:HS].rearrange("p g w t j d -> p (g w t j) d"),
                                     rs[:, :, :, :].rearrange("p g w x -> p (g w x)").unsqueeze(2).broadcast_to(
                                         [128, G * 2 * NT * J, HS]), ALU.mult).then_inc(s_pr, 1)
                    gp.wait_ge(s_pr, c + 1)
                    ge(gp, s_ln[1][4], c)
                    gp.tensor_tensor(o_t[:, :, :].rearrange("p t (g x) -> p g t x", g=G), prod[:, :, 0, :, :],
                                     prod[:, :, 1, :, :], ALU.subtract).then_inc(s_o, 1)
                    inverse_std(1, c)
                    normalise(1, c, on, o_t)
                    gp.wait_ge(s_ln[1][4], c + 1)
                    if isinstance(c, int) and c == 0:
                        gp.wait_ge(s_tabs, 16)
                    gp.tensor_tensor(og[:, :, :], on[:, :, :], tabs[:, ds(c), 0, :].broadcast_to([128, NT, C]),
                                     ALU.mult).then_inc(s_og, 1)
                    gp.wait_ge(s_og, c + 1)
                    gp.tensor_tensor(ob[:, :, :], og[:, :, :], tabs[:, ds(c), 1, :].broadcast_to([128, NT, C]),
                                     ALU.add).then_inc(s_ob, 1)
                    gp.wait_ge(s_ob, c + 1)
                    gp.tensor_tensor(x_all[:, ds(NT * c, NT), :], x_all[:, ds(NT * c, NT), :], ob[:, :, :],
                                     ALU.add).then_inc(s_xc, 1)

            def rows_out():
                gp.wait_ge(s_set, 20)
                gp.dma_start(rows_d[:, :], tab8[:, :, :].rearrange("b a c -> b (a c)")).then_inc(s_rows_d, 16)

            def rows_in():
                gp.wait_ge(s_rows_d, 16)
                gp.dma_start(tabs[:, :, :, :].rearrange("p b a c -> p (b a c)"),
                             rows_d.rearrange("b x -> (b x)").unsqueeze(0).broadcast_to([128, B * 6 * C])
                             ).then_inc(s_tabs, 16)
                gp.wait_ge(s_late, 16)
                gp.wait_ge(s_b2, 16 * B)
                for b in range(B):
                    ins = gp.tensor_scalar(b2m[:, b, :], b2t[:, :], wl("blocks", b, 1), None, ALU.mult)
                ins.then_inc(s_gs, 1)

            gp.wait_ge(s_xin, 16)
            run_loop(gp, body, rows_in, past=2, first=rows_out)

            def experts0(b, i, last=False):
                gp.wait_ge(s_zmv, b + 1)
                gp.tensor_tensor(zrs[:, i, :], zmv[:, i, :, 1], eps_c[:, :], ALU.add).then_inc(s_zeps, 1)
                gp.wait_ge(s_zeps, b + 1)
                gp.tensor_tensor(zrs[:, i, :], zrs[:, i, :], half[:, :], ALU.pow).then_inc(s_zrs, 1)
                gp.wait_ge(s_zn, b + 3)
                gp.tensor_tensor(zg[:, i, :, :], zn[:, i, :, :], tabs[:, ds(b), 2, :].broadcast_to([128, NT, C]),
                                 ALU.mult).then_inc(s_zg, 1)
                gp.wait_ge(s_zg, b + 1)
                gp.tensor_tensor(zb[:, i, :, :], zg[:, i, :, :], tabs[:, ds(b), 3, :].broadcast_to([128, NT, C]),
                                 ALU.add).then_inc(s_zb, 1)
                gp.wait_ge(s_zb, b + 1)
                gp.tensor_tensor(x_all[:, ds(NT * b, NT), :], x_all[:, ds(NT * b, NT), :], zb[:, i, :, :],
                                 ALU.add).then_inc(s_zx, 1)


            def inverse_std1(i, b):
                gp.wait_ge(c_ln[i][1], b + 1)
                gp.tensor_tensor(rstd1[i][:, :], meanvar1[i][:, :, 1], eps_c[:, :], ALU.add).then_inc(c_ln[i][2], 1)
                gp.wait_ge(c_ln[i][2], b + 1)
                gp.tensor_tensor(rstd1[i][:, :], rstd1[i][:, :], half[:, :], ALU.pow).then_inc(c_ln[i][3], 1)

            def spread_v1(b, part):
                gp.wait_ge(c_vs, b + 1)
                ge(gp, c_pv, 4 * b - 2 + 2 * part)
                hold(gp)
                hh = slice(8 * part, 8 * part + 8)
                gp.tensor_copy(v32[:, :, hh, 0:HS], vs[:, :, hh, :]).then_inc(c_vc, 1)

            def body1(b, ticks=range(H)):
                for u in ticks:
                    if has(b, 0):
                        n = 16 * b + u
                        gp.wait_ge(c_clip, n + 1)
                        ge(gp, c_exp, n - 3)
                        gp.tensor_tensor(dec[:, u % 4, :], clip[:, u % 2, :], wl("decay"), ALU.mult).then_inc(c_mul, 1)
                    if u == 0 and has(b, 1):
                        inverse_std1(0, b + 1)
                    if u == 5 and has(b, 0):
                        spread_v1(b, 0)
                    if u == 7 and has(b, 0):
                        spread_v1(b, 1)
                    if u == 10 and has(b, -1):
                        c = b - 1
                        gp.wait_ge(c_rc, c + 1)
                        ge(gp, c_oT, c)
                        for p in range(2):
                            for w in range(2):
                                g = 2 * p + w
                                ins = gp.tensor_tensor(
                                    o1[:, :, 32 * g:32 * g + 32].rearrange("p t (j d) -> p t j d", d=HS),
                                    ok1[:, p, w, :, :, 0:HS],
                                    rs1[:, p, w, :, :].unsqueeze(3).broadcast_to([128, NT, J, HS]), ALU.mult)
                        ins.then_inc(c_o, 1)
                    if u == 1 and has(b, -2):
                        c = b - 2
                        gp.wait_ge(c_yg, c + 1)
                        gp.tensor_tensor(x_all[:, ds(NT * c, NT), :], x_all[:, ds(NT * c, NT), :], yg[:, :, :],
                                         ALU.add).then_inc(c_x, 1)
                    if u == 4 and has(b, -2):
                        inverse_std1(1, b - 2)

            over_pairs(gp, experts0, body1)

            run_loop(gp, body1, past=2, started=True)
            gp.wait_ge(f_wtc, 4)
            for i in range(2):
                gp.tensor_copy(w9c[:, i, :], w9t[:, T * i:T * (i + 1)]).then_inc(f_wc, 1)
            with gp.Fori(1, B // 2) as pair:
                for i in range(2):
                    b = 2 * pair + i
                    gp.wait_ge(f_se, NT * (b - 1))
                    hold(gp)
                    gp.tensor_copy(w9c[:, i, :], w9t[:, ds(T * b, T)]).then_inc(f_wc, 1)

        @block.scalar
        def _(act):
            act.wait_ge(s_in, 16)
            nc.scalar.activation(silu_t[:, :], we("ct"), ACT.Exp, scale=-1.0).then_inc(s_seta, 1)

            def exp_fill(b, r, j):
                n = 32 * b + 4 * r + j
                act.wait_ge(s_b_full, n + 1)
                if j == 0:
                    ge(act, s_pv, 8 * b + r - 1)
                nc.scalar.activation(probs[:, r % 2, j, :], ps_b[j % 2][:, :], ACT.Exp,
                                     scale=SCALE0).then_inc(s_exp, 1)

            def copy_pv(b, g):
                act.wait_ge(s_pv, 8 * b + 2 * g + 2)
                ge(act, s_otr, 4 * b + g - 1)
                nc.scalar.activation(ot[:, g % 2, :], ps_pv[g % 2][:, :], ACT.Copy).then_inc(s_ot, 1)

            def copy_turned(b, g):
                act.wait_ge(s_otr, 4 * b + g + 1)
                if g == 0:
                    ge(act, s_pr, b)
                src = ps_m[1][:, :].rearrange("p (x j e) -> p x j e", j=J, e=32)[:, :, :, 0:HS + 1]
                nc.scalar.activation(ok[:, g, :, :, :, :].rearrange("p w t j d -> p (w t) j d"), src,
                                     ACT.Copy).then_inc(s_ok, 1)

            def copy_max(b, g):
                act.wait_ge(s_mtr, 4 * b + g + 1)
                ge(act, s_mrow[g], 16 * b)
                nc.scalar.activation(mrow[:, g, :], ps_m[0][0:8, :], ACT.Copy).then_inc(s_mcp, 1)

            def body(b):
                for u in range(8):
                    bb, off, r = b_round(b, u)
                    pb, poff, pr = pv_round(b, u)
                    for j in range(2):
                        if has(b, off):
                            exp_fill(bb, r, j)
                    if u == 0 and has(b, -1):
                        copy_max(b - 1, 3)
                    if u in (2, 4, 6) and has(b, 0):
                        copy_max(b, u // 2 - 1)
                    for j in range(2, 4):
                        if has(b, off):
                            exp_fill(bb, r, j)
                    if pr % 2 and has(b, poff):
                        copy_pv(pb, pr // 2)
                    if u % 2 and has(b, 0 if u == 7 else -1):
                        copy_turned(b if u == 7 else b - 1, (u + 1) // 2 % 4)
                    if u == 4 and has(b, -2):
                        act.wait_ge(s_h2p, b - 1)
                        nc.scalar.activation(h2t[:, ds(T * (b - 2), T)], ps_m[1][:, 0:T], ACT.Identity,
                                             scale=mod_c[:, 3, ds(b - 2)], bias=mod_c[:, 2, ds(b - 2)]).then_inc(s_h2, 1)
                    if u == 3 and has(b, 1):
                        act.wait_ge(s_xt, b + 2)
                        ge(act, s_v, b + 1)
                        nc.scalar.activation(ht[:, :], ps_m[0][:, 0:T], ACT.Identity, scale=mod_c[:, 1, ds(b + 1)],
                                             bias=mod_c[:, 0, ds(b + 1)]).then_inc(s_ht, 1)
                    if u == 5 and has(b, 1):
                        act.wait_ge(s_q, b + 2)
                        for g in range(G):
                            ge(act, s_st[g], 64 * (b + 1) + 16, 17)
                        nc.scalar.activation(hl[:, 2, :, :].rearrange("p w t -> p (w t)"), ps_m[0][:, :],
                                             ACT.Copy).then_inc(s_qhi, 1)
                        act.wait_ge(s_k, b + 2)
                        nc.scalar.activation(hl[:, 1, :, :].rearrange("p w t -> p (w t)"), ps_m[1][:, :],
                                             ACT.Copy).then_inc(s_khi, 1)
                    if u == 6 and has(b, 1):
                        act.wait_ge(s_v, b + 2)
                        ge(act, s_vc, 2 * b + 2)
                        nc.scalar.activation(vs[:, :, :, :].rearrange("p t h d -> p (t h d)"), ps_m[0][:, 0:T],
                                             ACT.Copy).then_inc(s_vs, 1)

            def gelu(n):
                f, c = n % NF0, n // NF0
                act.wait_ge(s_g, n + 1)
                nc.scalar.activation(h1[:, f, c * 512:(c + 1) * 512], ps_b[n % 2][:, :], ACT.Gelu,
                                     bias=wl("b1", f, 1)).then_inc(s_ge, 1)

            def before_last():
                act.wait_ge(c_wp, 1)
                nc.scalar.activation(wlat[:, :], ps_a[1][0:32, 0:C], ACT.Copy).then_inc(c_w, 1)
                act.wait_ge(s_late, 16)
                for n in range(3):
                    gelu(n)
                act.wait_ge(c_wp, 2)
                nc.scalar.activation(wrec[:, :], ps_a[1][:, C:3 * C], ACT.Copy).then_inc(c_w, 1)
                for n in range(3, EARLY_HIDDEN):
                    gelu(n)

            def spreading():
                nc.scalar.activation(spread[:, :].rearrange("p (r f) -> p r f", f=F0),
                                     ident.unsqueeze(2).broadcast_to([128, 128, F0]), ACT.Copy).then_inc(s_gs, 1)

            run_loop(act, body, past=2, first=spreading, last=before_last)

            act.wait_ge(s_r, 2)
            nc.scalar.activation(lg[:, :, :], lg[:, :, :], ACT.Exp).then_inc(s_rexp, 1)
            for n in range(EARLY_HIDDEN, 16):
                gelu(n)
            act.wait_ge(s_rt, 1)
            nc.scalar.activation(route[:, :], ps_a[1][:, 0:T], ACT.Copy).then_inc(s_rtc, 1)

            def copy_h2(b, i):
                nc.scalar.activation(h2c[:, i, :], h2t[:, ds(T * b, T)], ACT.Copy).then_inc(s_h2c, 1)

            def experts0(b, i, last=False):
                if not last:
                    act.wait_ge(s_zn, b + 2)
                    copy_h2(b + 1, 1 - i)


            def body1(b, ticks=range(H)):
                for u in ticks:
                    h, off = at(u, 3)
                    if has(b, off):
                        n = 16 * (b + off) + h
                        act.wait_ge(c_max, n + 1)
                        ge(act, c_pt, n - 1)
                        for t in range(NT):
                            ins = nc.scalar.activation(prob1[:, h % 2, t * T:(t + 1) * T], dec[:, h % 4, t * T:(t + 1) * T],
                                                       ACT.Exp, bias=negmax1[:, h % 4, t:t + 1])
                        ins.then_inc(c_exp, 1)
                    h, off = at(u, 4)
                    if has(b, off):
                        n = 16 * (b + off) + h
                        act.wait_ge(c_pt, n + 1)
                        if h % 4 == 0:
                            ge(act, c_pv, 4 * (b + off) + h // 4 - 1)
                        nc.scalar.activation(probt[:, h // 4 % 2, h % 4, :], ps_b[h % 2][:, :],
                                             ACT.Copy).then_inc(c_ev, 1)
                    for p, tick, off in ((0, 14, 0), (1, 6, -1)):
                        if u == tick and has(b, off):
                            c = b + off
                            act.wait_ge(c_pv, 4 * c + 2 * p + 2)
                            ge(act, c_otr, 2 * c + p - 1)
                            nc.scalar.activation(ot1[:, p, :], ps_pv[p][:, :], ACT.Copy).then_inc(c_ot, 1)
                    for p, tick in ((0, 3), (1, 9)):
                        if u == tick and has(b, -1):
                            c = b - 1
                            act.wait_ge(c_otr, 2 * c + p + 1)
                            if p == 0:
                                ge(act, c_o, c)
                            src = ps_m[1][:, :].rearrange("p (x j e) -> p x j e", j=J, e=32)[:, :, :, 0:HS + 1]
                            nc.scalar.activation(ok1[:, p, :, :, :, :].rearrange("p w t j d -> p (w t) j d"), src,
                                                 ACT.Copy).then_inc(c_ok, 1)
                    if u == 10 and has(b, -2):
                        act.wait_ge(c_h4p, b - 1)
                        nc.scalar.activation(h2t[:, ds(T * (b - 2), T)], ps_m[0][:, 0:T], ACT.Identity,
                                             scale=mod_c[:, 7, ds(b - 2)], bias=mod_c[:, 6, ds(b - 2)]).then_inc(c_h4, 1)
                    if u == 5 and has(b, 1):
                        act.wait_ge(c_xt, b + 2)
                        ge(act, c_v, b + 1)
                        nc.scalar.activation(ht1[:, :], ps_m[0][:, 0:T], ACT.Identity, scale=mod_c[:, 5, ds(b + 1)],
                                             bias=mod_c[:, 4, ds(b + 1)]).then_inc(c_ht, 1)
                    if u == 7 and has(b, 1):
                        act.wait_ge(c_qk, b + 2)
                        for g in range(G):
                            ge(act, c_st[g], 64 * (b + 1))
                        nc.scalar.activation(hl1[:, 2, :], ps_m[0][:, 0:T], ACT.Copy).then_inc(c_qhi, 1)
                        nc.scalar.activation(hl1[:, 1, :], ps_m[0][:, T:2 * T], ACT.Copy).then_inc(c_khi, 1)
                    if u == 12 and has(b, 1):
                        act.wait_ge(c_v, b + 2)
                        ge(act, c_vc, 2 * b + 2)
                        nc.scalar.activation(vs[:, :, :, :].rearrange("p t h d -> p (t h d)"), ps_m[0][:, 0:T],
                                             ACT.Copy).then_inc(c_vs, 1)
                    if u == 14 and has(b, -1):
                        act.wait_ge(c_oT, b)
                        ge(act, c_y, b - 1)
                        nc.scalar.activation(o1t[:, :], ps_m[0][:, 0:T], ACT.Copy).then_inc(c_ots, 1)

            def gelus(c, i, f2):
                n = 9 * c + f2
                act.wait_ge(f_h, n + 1)
                for k in range(2):
                    f = 2 * f2 + k
                    ins = nc.scalar.activation(hid[:, i, f, :], ps_b[(i + f2) % 2][:, k * T:(k + 1) * T], ACT.Gelu,
                                               bias=wl("b1b", f, 1))
                ins.then_inc(f_ge, 1)

            def high1(c, i):
                nc.scalar.activation(h4s[:, i, 0, :], h2t[:, ds(T * c, T)], ACT.Copy).then_inc(f_xh, 1)

            def before_last1():
                act.wait_ge(c_ev, 16 * B)
                high1(0, 0)
                high1(1, 1)
                for f2 in range(NF1 // 2):
                    gelus(0, 0, f2)

            act.wait_ge(s_h2, B)
            copy_h2(0, 0)
            over_pairs(act, experts0, body1)

            def w1_high():
                act.wait_ge(s_zx, B)
                nc.scalar.activation(w1s[:, 0, :], wl("w1b"), ACT.Copy).then_inc(f_w1h, 1)

            run_loop(act, body1, past=2, first=w1_high, started=True, last=before_last1)

            act.wait_ge(f_r, 2)
            nc.scalar.activation(lg1[:, :, :], lg1[:, :, :], ACT.Exp).then_inc(f_exp, 1)
            for f2 in range(NF1 // 2):
                gelus(1, 1, f2)
            for i in range(4):
                act.wait_ge(f_wt, i + 1)
                nc.scalar.activation(w9t[:, 512 * i:512 * (i + 1)], ps_pv[i % 2][0:E1 + 1, :],
                                     ACT.Copy).then_inc(f_wtc, 1)

            high1(2, 0)
            high1(3, 1)
            with act.Fori(1, B // 2 - 1) as pair:
                for i in range(2):
                    for f2 in range(NF1 // 2):
                        gelus(2 * pair + i, i, f2)
                    high1(2 * pair + i + 2, i)
            for i in range(2):
                for f2 in range(NF1 // 2):
                    gelus(B - 2 + i, i, f2)

        @block.vector
        def _(dve):
            steps = [0]

            def link(ins):
                steps[0] += 1
                ins.then_inc(s_set, 1)
                dve.wait_ge(s_set, steps[0])

            nc.vector.memset(stack[:, 0:2, :, :, :].bitcast(F32), 0.0).then_inc(s_const, 1)
            nc.vector.memset(stack[:, 2:4, :, :, :].bitcast(F32), 0.0).then_inc(s_const, 1)
            dve.wait_ge(s_seta, 1)
            link(nc.vector.tensor_scalar(silu_t[:, :], silu_t[:, :], 1.0, None, ALU.add))
            link(nc.vector.reciprocal(silu_t[:, :], silu_t[:, :]))
            link(nc.vector.tensor_tensor(silu[:, :], silu_t[:, :], we("ct"), ALU.mult))
            dve.wait_ge(s_setp, 1)
            mods = ps_m[0][:, 0:8 * B].rearrange("p (k b) -> p k b", b=B)
            link(nc.vector.tensor_copy(mod_c[:, 0::2, :], mods[:, 0::2, :]))
            link(nc.vector.tensor_scalar(mod_c[:, 1::2, :], mods[:, 1::2, :], 1.0, None, ALU.add))
            def gates():
                dve.wait_ge(s_setp, 2)
                flat = lambda t: t[:, :, :].rearrange("p a c -> p (a c)")
                link(nc.vector.tensor_copy(flat(gate8), ps_a[0][0:8, :]))
                link(nc.vector.tensor_scalar(flat(gpos), flat(gate8), 0.0, None, ALU.is_ge))
                link(nc.vector.tensor_scalar(flat(gmax), flat(gate8), 0.25, None, ALU.max))
                link(nc.vector.tensor_tensor(flat(gmax), flat(gmax), flat(gpos), ALU.mult))
                link(nc.vector.tensor_scalar(flat(gate8), flat(gate8), -0.25, None, ALU.min))
                link(nc.vector.tensor_scalar(flat(gpos), flat(gpos), -1.0, 1.0, ALU.mult, ALU.add))
                link(nc.vector.tensor_tensor(flat(gate8), flat(gate8), flat(gpos), ALU.mult))
                link(nc.vector.tensor_tensor(flat(gate8), flat(gate8), flat(gmax), ALU.add))
                dve.wait_ge(s_setp, 4)
                link(nc.vector.tensor_copy(lam_c[:, 0:1], ps_b[0][:, 0:1]))
                link(nc.vector.tensor_scalar(lam_c[:, 1:2], lam_c[:, 0:1], -1.0, 1.0, ALU.mult, ALU.add))
                link(nc.vector.tensor_copy(flat(gam8), ps_a[1][0:8, :]))
                link(nc.vector.tensor_tensor(tab8[:, 0:2, :], gam8[:, 0:2, :], gate8[:, 0:1, :].broadcast_to([8, 2, C]),
                                             ALU.mult))
                link(nc.vector.tensor_scalar(tab8[:, 0:2, :], tab8[:, 0:2, :], lam_c[0:8, 1:2], None, ALU.mult))
                link(nc.vector.tensor_tensor(tab8[:, 2:4, :], gam8[:, 2:4, :], gate8[:, 1:2, :].broadcast_to([8, 2, C]),
                                             ALU.mult))
                link(nc.vector.tensor_copy(tab8[:, 4:6, :], gate8[:, 2:4, :]))
                assert steps[0] == 20

            def ln_stats(i, b, src):
                for t in range(NT):
                    ins = nc.vector.bn_stats(stats[i][:, t, :], src(t))
                ins.then_inc(s_ln[i][0], 1)
                dve.wait_ge(s_ln[i][0], b + 1)
                hold(dve)
                for t in range(NT):
                    ins = nc.vector.bn_aggr(meanvar[i][:, t, :], stats[i][:, t, :])
                ins.then_inc(s_ln[i][1], 1)

            def take_max(b, u, j):
                n = 32 * b + 4 * u + j
                dve.wait_ge(s_a_full, n + 1)
                nc.vector.tensor_reduce(negmax[:, u // 2, u % 2, :, j],
                                        ps_a[j % 2][:, :].rearrange("p (t k) -> p t k", t=NT), AX.X, ALU.max,
                                        negate=True).then_inc(s_a_max, 1)

            def split_max(b, g):
                dve.wait_ge(s_a_max, 32 * b + 8 * g + 8)
                ge(dve, s_mtr, 4 * b + g - 3)
                src = negmax[:, g, :, :, :].rearrange("p w t j -> p (w t) j")
                nc.vector.tensor_copy(mhl[:, g, :, :, 0], src).then_inc(s_mhi, 1)
                dve.wait_ge(s_mhi, 4 * b + g + 1)
                nc.vector.tensor_tensor(mhl[:, g, :, :, 1], src, mhl[:, g, :, :, 0].bitcast(F32),
                                        ALU.subtract).then_inc(s_mlo, 1)

            def low_part(bank, hi, lo):
                nc.vector.tensor_tensor(hl[:, lo, :, :].rearrange("p w t -> p (w t)"), ps_m[bank][:, :],
                                        hl[:, hi, :, :].rearrange("p w t -> p (w t)").bitcast(F32),
                                        ALU.subtract).then_inc([s_qlo, s_klo][bank], 1)

            def body(b):
                for u in range(8):
                    if has(b, 0):
                        for j in range(4):
                            take_max(b, u, j)
                        if u % 2:
                            split_max(b, u // 2)
                    if u == 0 and has(b, 1):
                        ge(dve, s_ln[0][4], b + 1)
                        ln_stats(0, b + 1, lambda t: x_all[:, ds(NT * (b + 1) + t), :].rearrange("p a c -> p (a c)"))
                    if u == 2 and has(b, -2):
                        c = b - 2
                        dve.wait_ge(s_xc, c + 1)
                        ge(dve, s_ln[2][4], c)
                        ln_stats(2, c, lambda t: x_all[:, ds(NT * c + t), :].rearrange("p a c -> p (a c)"))
                    if u == 4 and has(b, -2):
                        c = b - 2
                        dve.wait_ge(s_ln[2][3], c + 1)
                        ge(dve, s_h2p, c)
                        for t in range(NT):
                            ins = nc.vector.tensor_scalar(xn2[:, t, :].unsqueeze(1), x_all[:, ds(NT * c + t), :],
                                                          meanvar[2][:, t, 0:1], rstd[2][:, t:t + 1], ALU.subtract,
                                                          ALU.mult)
                        ins.then_inc(s_ln[2][4], 1)
                    if u == 2 and has(b, 1):
                        dve.wait_ge(s_ln[0][3], b + 2)
                        ge(dve, s_xt, b + 1)
                        for t in range(NT):
                            ins = nc.vector.tensor_scalar(xn1[:, t, :].unsqueeze(1), x_all[:, ds(NT * (b + 1) + t), :],
                                                          meanvar[0][:, t, 0:1], rstd[0][:, t:t + 1], ALU.subtract,
                                                          ALU.mult)
                        ins.then_inc(s_ln[0][4], 1)
                    if u == 6 and has(b, -1):
                        c = b - 1
                        dve.wait_ge(s_ok, 4 * c + 4)
                        ge(dve, s_pr, c)
                        nc.vector.reciprocal(rs[:, :, :, :].rearrange("p g w x -> p (g w x)"),
                                             ok[:, :, :, :, :, HS].rearrange("p g w t j -> p (g w t j)")
                                             ).then_inc(s_rc, 1)
                        dve.wait_ge(s_rc, 2 * c + 1)
                        nc.vector.tensor_scalar(rs[:, :, 1, :], rs[:, :, 1, :], lam_c[:, 0:1], None,
                                                ALU.mult).then_inc(s_rc, 1)
                    if u == 5 and has(b, 1):
                        dve.wait_ge(s_qhi, b + 2)
                        low_part(0, 2, 0)
                        dve.wait_ge(s_khi, b + 2)
                        low_part(1, 1, 3)
                    if u == 7 and has(b, -1):
                        dve.wait_ge(s_o, b)
                        ge(dve, s_ln[1][4], b - 1)
                        ln_stats(1, b - 1, lambda t: o_t[:, t, :])

            def fold():
                dve.wait_ge(s_late, 16)
                nc.vector.tensor_tensor(wkv[:, :], wl("wkt"), wl("wvt"), ALU.add).then_inc(c_w, 1)

            dve.wait_ge(s_xin, 16)
            run_loop(dve, body, past=2, first=gates, aside=fold)

            steps[0] = 0

            def step(ins):
                steps[0] += 1
                ins.then_inc(s_r, 1)
                dve.wait_ge(s_r, steps[0])

            over = lambda t: t[:, :].unsqueeze(2).broadcast_to([128, B * NT, E0])
            flat2 = lambda t: t[:, :, :].rearrange("p a e -> p (a e)")
            iota = wl("iota").unsqueeze(1).broadcast_to([128, B * NT, E0])
            dve.wait_ge(s_lg, 2)
            logits = ps_a[0][:, 0:B * NT * E0].rearrange("p (a e) -> p a e", e=E0)
            step(nc.vector.tensor_reduce(col[0][:, :], logits, AX.X, ALU.max))
            step(nc.vector.tensor_tensor(lg[:, :, :], logits, over(col[0]), ALU.subtract))
            dve.wait_ge(s_rexp, 1)
            dve.wait_ge(s_late, 16)
            step(nc.vector.tensor_reduce(col[0][:, :], lg[:, :, :], AX.X, ALU.add))
            step(nc.vector.reciprocal(col[0][:, :], col[0][:, :]))
            step(nc.vector.tensor_tensor(lg[:, :, :], lg[:, :, :], over(col[0]), ALU.mult))
            for k in range(2):
                src = [lg, sc][k]
                step(nc.vector.tensor_reduce(col[0][:, :], src[:, :, :], AX.X, ALU.max))
                step(nc.vector.tensor_tensor(eq[:, :, :], src[:, :, :], over(col[0]), ALU.is_equal))
                step(nc.vector.scalar_tensor_tensor(key[:, :, :], eq[:, :, :], -64.0, iota, ALU.mult, ALU.add))
                step(nc.vector.tensor_reduce(col[1][:, :], key[:, :, :], AX.X, ALU.min))
                step(nc.vector.tensor_tensor([pick, eq][k][:, :, :], key[:, :, :], over(col[1]), ALU.is_equal))
                if k == 0:
                    step(nc.vector.scalar_tensor_tensor(flat2(sc), flat2(pick), -4.0, flat2(lg), ALU.mult, ALU.add))
            step(nc.vector.tensor_tensor(flat2(pick), flat2(pick), flat2(eq), ALU.add))
            step(nc.vector.tensor_tensor(flat2(pick), flat2(pick), flat2(lg), ALU.mult))
            step(nc.vector.tensor_reduce(den[:, :], pick[:, :, :].rearrange("p (b t) e -> p (t e) b", t=NT), AX.X,
                                         ALU.add))
            step(nc.vector.tensor_scalar(den[:, :], den[:, :], 1e-6, None, ALU.add))
            step(nc.vector.reciprocal(den[:, :], den[:, :]))
            step(nc.vector.tensor_scalar(den[:, :], den[:, :], float(B), None, ALU.mult))
            step(nc.vector.tensor_tensor(rt[:, :, :, :].rearrange("p t b e -> p b t e"),
                                         pick[:, :, :].rearrange("p (b t) e -> p b t e", t=NT),
                                         den[:, :].rearrange("p (t e) -> p t e", e=E0).unsqueeze(1).broadcast_to(
                                             [128, B, NT, E0]), ALU.mult))
            n_route = steps[0]
            assert n_route == 23, n_route
            dve.wait_ge(s_rtc, 1)
            for k in range(T // 2 // 8):
                step(nc.vector.max(top8[:, :], route[:, :]))
                step(nc.vector.match_replace(out=route[:, :], in_to_replace=top8[:, :], in_values=route[:, :],
                                             imm_value=-1.0))
            step(nc.vector.tensor_scalar(selb[:, :], route[:, :], -1.0, None, ALU.is_equal))
            step(nc.vector.tensor_scalar(sel[:, :], route[:, :], -1.0, None, ALU.is_equal))

            def mask_hidden(b, i):
                dve.wait_ge(s_mask, b + 1)
                for f in range(0, NF0, 2):
                    ins = nc.vector.tensor_tensor(hm[:, i, f:f + 2, :], h1[:, f:f + 2, ds(T * b, T)],
                                                  [ps_a, ps_b][i][f // 2][:, :].rearrange("p (f t) -> p f t", f=2),
                                                  ALU.mult)
                ins.then_inc(s_hm, 1)

            def experts0(b, i, last=False):
                if not last:
                    mask_hidden(b + 1, 1 - i)
                dve.wait_ge(s_z, b + 1)
                for t in range(NT):
                    ins = nc.vector.bn_stats(zst[:, i, t, :], ps_pv[i][:, t * C:(t + 1) * C])
                ins.then_inc(s_zst, 1)
                dve.wait_ge(s_zst, b + 1)
                hold(dve)
                for t in range(NT):
                    ins = nc.vector.bn_aggr(zmv[:, i, t, :], zst[:, i, t, :])
                ins.then_inc(s_zmv, 1)
                dve.wait_ge(s_zrs, b + 1)
                for t in range(NT):
                    ins = nc.vector.tensor_scalar(zn[:, i, t, :], ps_pv[i][:, t * C:(t + 1) * C],
                                                  zmv[:, i, t, 0:1], zrs[:, i, t:t + 1], ALU.subtract, ALU.mult)
                ins.then_inc(s_zn, 1)

            dve.wait_ge(s_ge, 16)
            nc.vector.memset(spare[:, 0:1], 0.0).then_inc(s_zn, 2)
            mask_hidden(0, 0)

            def ln_stats1(i, b):
                for t in range(NT):
                    ins = nc.vector.bn_stats(stats1[i][:, t, :],
                                             x_all[:, ds(NT * b + t), :].rearrange("p a c -> p (a c)"))
                ins.then_inc(c_ln[i][0], 1)
                dve.wait_ge(c_ln[i][0], b + 1)
                hold(dve)
                for t in range(NT):
                    ins = nc.vector.bn_aggr(meanvar1[i][:, t, :], stats1[i][:, t, :])
                ins.then_inc(c_ln[i][1], 1)

            def normalise1(i, b, dst):
                dve.wait_ge(c_ln[i][3], b + 1)
                for t in range(NT):
                    ins = nc.vector.tensor_scalar(dst[:, t, :].unsqueeze(1), x_all[:, ds(NT * b + t), :],
                                                  meanvar1[i][:, t, 0:1], rstd1[i][:, t:t + 1], ALU.subtract, ALU.mult)
                ins.then_inc(c_ln[i][4], 1)

            def body1(b, ticks=range(H)):
                for u in ticks:
                    if has(b, 0):
                        n = 16 * b + u
                        dve.wait_ge(c_s, n + 1)
                        ge(dve, c_mul, n - 1)
                        nc.vector.tensor_scalar(clip[:, u % 2, :], ps_a[u % 2][:, :], -CLAMP / SCALE1, CLAMP / SCALE1,
                                                ALU.max, ALU.min).then_inc(c_clip, 1)
                    h, off = at(u, 2)
                    if has(b, off):
                        n = 16 * (b + off) + h
                        dve.wait_ge(c_mul, n + 1)
                        ge(dve, c_exp, n - 3)
                        nc.vector.tensor_reduce(negmax1[:, h % 4, :], dec[:, h % 4, :].rearrange("p (t k) -> p t k", t=NT),
                                                AX.X, ALU.max, negate=True).then_inc(c_max, 1)
                    if u == 0 and has(b, 1):
                        dve.wait_ge(s_zx, b + 2)
                        ge(dve, c_ln[0][4], b + 1)
                        ln_stats1(0, b + 1)
                    if u == 2 and has(b, 1):
                        ge(dve, c_xt, b + 1)
                        normalise1(0, b + 1, xn3)
                    if u == 10 and has(b, -1):
                        dve.wait_ge(c_ok, 2 * b)
                        ge(dve, c_o, b - 1)
                        nc.vector.reciprocal(rs1[:, :, :, :, :].rearrange("p a w t j -> p (a w t j)"),
                                             ok1[:, :, :, :, :, HS].rearrange("p a w t j -> p (a w t j)")
                                             ).then_inc(c_rc, 1)
                    if u == 8 and has(b, 1):
                        dve.wait_ge(c_khi, b + 2)
                        for lo, hi, part in ((0, 2, 0), (3, 1, 1)):
                            ins = nc.vector.tensor_tensor(hl1[:, lo, :], ps_m[0][:, part * T:(part + 1) * T],
                                                          hl1[:, hi, :].bitcast(F32), ALU.subtract)
                        ins.then_inc(c_lo, 1)
                    if u == 0 and has(b, -2):
                        dve.wait_ge(c_y, b - 1)
                        ge(dve, c_x, b - 2)
                        nc.vector.tensor_tensor(yg[:, :, :], ps_m[1][:, 0:T].rearrange("p (t c) -> p t c", t=NT),
                                                tabs[:, ds(b - 2), 4, :].broadcast_to([128, NT, C]),
                                                ALU.mult).then_inc(c_yg, 1)
                    if u == 3 and has(b, -2):
                        dve.wait_ge(c_x, b - 1)
                        ge(dve, c_ln[1][4], b - 2)
                        ln_stats1(1, b - 2)
                    if u == 6 and has(b, -2):
                        ge(dve, c_h4p, b - 2)
                        normalise1(1, b - 2, xn4)

            over_pairs(dve, experts0, body1)

            def low1(c, i):
                dve.wait_ge(f_xh, c + 1)
                nc.vector.tensor_tensor(h4s[:, i, 1, :], h2t[:, ds(T * c, T)], h4s[:, i, 0, :].bitcast(F32),
                                        ALU.subtract).then_inc(f_xl, 1)

            def before_last1():
                low1(0, 0)
                low1(1, 1)

            def w1_low():
                dve.wait_ge(f_w1h, 1)
                nc.vector.tensor_tensor(w1s[:, 1, :], wl("w1b"), w1s[:, 0, :].bitcast(F32),
                                        ALU.subtract).then_inc(f_w1l, 1)

            run_loop(dve, body1, past=2, aside=w1_low, started=True, last=before_last1)

            steps[0] = 0

            def step1(ins):
                steps[0] += 1
                ins.then_inc(f_r, 1)
                dve.wait_ge(f_r, steps[0])

            over1 = lambda t: t[:, :].unsqueeze(2).broadcast_to([128, B * NT, E1])
            iota1 = wl("iota", 0, E1).unsqueeze(1).broadcast_to([128, B * NT, E1])
            dve.wait_ge(f_lg, 2)
            logits = ps_a[0][:, 0:B * NT * E1].rearrange("p (a e) -> p a e", e=E1)
            step1(nc.vector.tensor_reduce(cols1[0][:, :], logits, AX.X, ALU.max))
            step1(nc.vector.tensor_tensor(lg1[:, :, :], logits, over1(cols1[0]), ALU.subtract))
            dve.wait_ge(f_exp, 1)
            step1(nc.vector.tensor_reduce(cols1[0][:, :], lg1[:, :, :], AX.X, ALU.add))
            step1(nc.vector.reciprocal(cols1[0][:, :], cols1[0][:, :]))
            step1(nc.vector.tensor_tensor(lg1[:, :, :], lg1[:, :, :], over1(cols1[0]), ALU.mult))
            for k in range(2):
                src = [lg1, sc1][k]
                step1(nc.vector.tensor_reduce(cols1[0][:, :], src[:, :, :], AX.X, ALU.max))
                step1(nc.vector.tensor_tensor(eq1[:, :, :], src[:, :, :], over1(cols1[0]), ALU.is_equal))
                step1(nc.vector.scalar_tensor_tensor(key1[:, :, :], eq1[:, :, :], -64.0, iota1, ALU.mult, ALU.add))
                step1(nc.vector.tensor_reduce(cols1[1][:, :], key1[:, :, :], AX.X, ALU.min))
                step1(nc.vector.tensor_tensor([pick1, eq1][k][:, :, :], key1[:, :, :], over1(cols1[1]), ALU.is_equal))
                if k == 0:
                    step1(nc.vector.scalar_tensor_tensor(flat2(sc1), flat2(pick1), -4.0, flat2(lg1), ALU.mult, ALU.add))
            step1(nc.vector.tensor_tensor(flat2(pick1), flat2(pick1), flat2(eq1), ALU.add))
            step1(nc.vector.tensor_tensor(w9[:, :, 0:E1], pick1[:, :, :], lg1[:, :, :], ALU.mult))
            step1(nc.vector.memset(w9[:, :, E1:E1 + 1], 1.0))
            assert steps[0] == W9_STEPS, steps[0]

            nc.vector.memset(acc[:, :, :, :], 0.0).then_inc(f_acc, ACC_STEPS * NT)
            dve.wait_ge(f_acc, ACC_STEPS * NT)

            def token_tile(c, i, t):
                base = ACC_STEPS * (NT * (c + 1) + t)
                k = [0]
                w = lambda e: w9[:, ds(NT * c + t), e]
                tile = lambda a: a.unsqueeze(1)

                def link1(ins):
                    k[0] += 1
                    ins.then_inc(f_acc, 1)

                def then():
                    dve.wait_ge(f_acc, base + k[0])

                dve.wait_ge(f_se, NT * c + t + 1)
                expert = lambda e: [[ps_a[0], ps_a[1]], [ps_m[0], ps_m[1]]][t][e // 4][:, e % 4 * C:(e % 4 + 1) * C]
                link1(nc.vector.tensor_scalar(acc[:, t, 0, :], expert(0), w(0), None, ALU.mult))
                for e in range(1, E1):
                    then()
                    link1(nc.vector.scalar_tensor_tensor(acc[:, t, e % 2, :], expert(e), w(e), acc[:, t, 1 - e % 2, :],
                                                         ALU.mult, ALU.add))
                then()
                link1(nc.vector.tensor_tensor(acc[:, t, 0, :], acc[:, t, 1, :], ps_pv[t][:, 0:C], ALU.add))
                then()
                link1(nc.vector.tensor_tensor(tile(acc[:, t, 1, :]), tile(acc[:, t, 0, :]), tabs[:, ds(c), 5, :], ALU.mult))
                then()
                link1(nc.vector.tensor_tensor(x_all[:, ds(NT * c + t), :], tile(acc[:, t, 1, :]), x_all[:, ds(NT * c + t), :],
                                              ALU.add))
                assert k[0] == ACC_STEPS

            def batch1(c, i):
                for t in range(NT):
                    token_tile(c, i, t)

            with dve.Fori(0, B // 2 - 1) as pair:
                for i in range(2):
                    low1(2 * pair + i + 2, i)
                    batch1(2 * pair + i, i)
            for i in range(2):
                batch1(B - 2 + i, i)

        @block.tensor
        def _(pe):
            mm = nc.tensor.matmul
            pe.wait_ge(s_in, 16)
            pe.wait_ge(s_set, 3)
            for l in range(2):
                for i, chunk in enumerate((0, 1, 3, 4)):
                    k = 4 * l + i
                    ins = mm(ps_m[0][:, k * B:(k + 1) * B], we(f"wmod{l}", chunk * C, C), silu[:, l * B:(l + 1) * B],
                             start=True, stop=True)
            ins.then_inc(s_setp, 1)
            for l in range(2):
                for i, chunk in enumerate((2, 5)):
                    k = 2 * l + i
                    ins = mm(ps_a[0][0:8, k * C:(k + 1) * C], silu[:, l * B:(l + 1) * B], we(f"wmod{l}", chunk * C, C),
                             start=True, stop=True)
            ins.then_inc(s_setp, 1)
            pe.wait_ge(s_rows, 16)
            pe.wait_ge(s_const, 4)
            mm(ps_a[1][0:8, :], ones[0:1, 0:8], wr("gammas"), start=True, stop=True).then_inc(s_setp, 1)
            mm(ps_b[0][:, 0:1], ones[0:1, 0:128], wr("lamb"), start=True, stop=True).then_inc(s_setp, 1)
            pe.wait_ge(s_set, 5)

            def keep_warm(bank):
                mm(bank[:, :], spread[:, 0:128], spread[:, 0:512], start=True, stop=True)

            def a_fill(b, u, j):
                n, g, w = 32 * b + 4 * u + j, u // 2, u % 2
                if w == 0 and j == 0:
                    pe.wait_ge(s_st[g], 64 * (b + 1) + 16)
                ge(pe, s_a_max, n - 1)
                if j == 0:
                    keep_warm(ps_a[0])
                rows_j = slice(32 * j, 32 * j + 32)
                for t in range(NT):
                    ins = mm(ps_a[j % 2][:, t * T:(t + 1) * T], stack[rows_j, g, 0, w, t * 128:(t + 1) * 128],
                             stack[rows_j, g, 1, w, :], start=True, stop=True)
                ins.then_inc(s_a_full, 1)

            def b_fill(b, r, j):
                n, g, w = 32 * b + 4 * r + j, r // 2, r % 2
                if w == 0 and j == 0:
                    pe.wait_ge(s_mrow[g], 16 * (b + 1))
                ge(pe, s_exp, n - 1)
                rows_j = slice(32 * j, 32 * j + 32)
                for t in range(NT):
                    ins = mm(ps_b[j % 2][:, t * T:(t + 1) * T], stack[rows_j, g, 1, w, t * 128:(t + 1) * 128],
                             stack[rows_j, g, 0, w, :], start=True, stop=True)
                ins.then_inc(s_b_full, 1)

            def pv(b, r):
                g, w = r // 2, r % 2
                pe.wait_ge(s_exp, 32 * b + 4 * r + 4)
                pe.wait_ge(s_vc, 2 * b + 1 + g // 2)
                if w == 0:
                    ge(pe, s_ot, 4 * b + g - 1)
                for t in range(NT):
                    for j in range(J):
                        ins = mm(ps_pv[g % 2][32 * j:32 * j + 32, w * T:(w + 1) * T], v32[:, t, J * g + j, :],
                                 probs[:, r % 2, j, t * T:(t + 1) * T], start=(t == 0), stop=(t == NT - 1))
                ins.then_inc(s_pv, 1)

            def turn_max(b, g, it):
                wait_emptied(pe, 0, f"mT{g}", it)
                pe.wait_ge(s_mlo, 4 * b + g + 1)
                for x_ in range(2 * NT):
                    ins = nc.tensor.transpose(ps_m[0][0:8, x_ * 128:(x_ + 1) * 128],
                                              mhl[:, g, x_, :, :].rearrange("p j s -> p (j s)").bitcast(F32), ident)
                ins.then_inc(s_mtr, 1)

            def turn_pv(b, g, it):
                wait_emptied(pe, 1, f"oT{g}", it)
                pe.wait_ge(s_ot, 4 * b + g + 1)
                for x_ in range(2 * NT):
                    ins = nc.tensor.transpose(ps_m[1][:, x_ * 128:(x_ + 1) * 128],
                                              ot[:, g % 2, x_ * 128:(x_ + 1) * 128], ident)
                ins.then_inc(s_otr, 1)

            def turn(bank, src, s):
                for t in range(NT):
                    ins = nc.tensor.transpose(ps_m[bank][:, t * 128:(t + 1) * 128], src[:, t, :], ident)
                ins.then_inc(s, 1)

            def project(bank, first, s):
                for w in range(2):
                    ins = mm(ps_m[bank][:, w * T:(w + 1) * T], we("wqk0", (first + w) * C, C), ht[:, :],
                             start=True, stop=True)
                ins.then_inc(s, 1)

            def body(b):
                for u in range(8):
                    bb, off, r = b_round(b, u)
                    pb, poff, pr = pv_round(b, u)
                    for j in range(4):
                        if j == 1 and has(b, poff):
                            pv(pb, pr)
                        if j == 3 and u % 2 and has(b, 0 if u == 7 else -1):
                            g = (u + 1) // 2 % 4
                            turn_pv(b if u == 7 else b - 1, g, b)
                        if j == 2:
                            if u == 0 and has(b, -1):
                                turn_max(b - 1, 3, b)
                            if u in (2, 4, 6) and has(b, 0):
                                turn_max(b, u // 2 - 1, b)
                        if has(b, 0):
                            a_fill(b, u, j)
                        if has(b, off):
                            b_fill(bb, r, j)
                    if u == 4 and has(b, -2):
                        wait_emptied(pe, 1, "h2T", b)
                        pe.wait_ge(s_ln[2][4], b - 1)
                        turn(1, xn2, s_h2p)
                    if u == 3 and has(b, 1):
                        wait_emptied(pe, 0, "xT", b)
                        pe.wait_ge(s_ln[0][4], b + 2)
                        turn(0, xn1, s_xt)
                    if u == 5 and has(b, 1):
                        pe.wait_ge(s_ht, b + 2)
                        wait_emptied(pe, 0, "q", b)
                        project(0, 0, s_q)
                        wait_emptied(pe, 1, "k", b)
                        project(1, 2, s_k)
                    if u == 6 and has(b, 1):
                        wait_emptied(pe, 0, "v", b)
                        for t in range(NT):
                            ins = mm(ps_m[0][:, t * C:(t + 1) * C], ht[:, t * 128:(t + 1) * 128], we("wv0"),
                                     start=True, stop=True)
                        ins.then_inc(s_v, 1)

            def warm_up(bank, n):
                for _ in range(n):
                    mm(bank[:, :], ones[:, 0:128], ones[:, :], start=True, stop=True)

            def before_first():
                warm_up(ps_b[1], 5)
                pe.wait_ge(s_set, 20)
                pe.wait_ge(s_gs, 1)

            def hidden(n):
                f, c = n % NF0, n // NF0
                if n < 2:
                    pe.wait_ge(s_exp, 32 * B)
                    pe.wait_ge(s_pv, 8 * B)
                    pe.wait_ge(s_late, 16)
                ge(pe, s_ge, n - 1)
                pe.wait_ge(s_h2, 2 * c + 2)
                mm(ps_b[n % 2][:, :], wl("w1", f * 128, 128), h2t[:, c * 512:(c + 1) * 512], start=True,
                   stop=True).then_inc(s_g, 1)

            def bias_rows(row, n):
                mm(ps_a[0][:, 0:B * NT * n], ones[0:1, 0:128], row.unsqueeze(1).broadcast_to([1, B * NT, n]),
                   start=True, stop=False)

            def logits(lo, hi):
                for t in range(lo, hi):
                    ins = mm(ps_a[0][:, t * E0:(t + 1) * E0], h2t[:, t * 128:(t + 1) * 128], wl("wg"),
                             start=False, stop=(t == B * NT - 1))
                ins.then_inc(s_lg, 1)

            def before_last():
                pe.wait_ge(s_small, 32)
                pe.wait_ge(s_a_max, 32 * B)
                pe.wait_ge(c_w, 1)
                mm(ps_a[1][0:32, 0:C], wl("wdown"), wkv[:, :], start=True, stop=True).then_inc(c_wp, 1)
                for n in range(3):
                    hidden(n)
                pe.wait_ge(c_w, 2)
                mm(ps_a[1][:, C:3 * C], wlat[:, :], wup_s[:, :], start=True, stop=True).then_inc(c_wp, 1)
                for n in range(3, EARLY_HIDDEN):
                    hidden(n)
                bias_rows(wr("bg"), E0)
                logits(0, NT * (B - 2))

            run_loop(pe, body, past=2, first=before_first, last=before_last)

            pe.wait_ge(s_h2, B)
            logits(NT * (B - 2), NT * B)
            for n in range(EARLY_HIDDEN, 16):
                hidden(n)
            pe.wait_ge(c_w, 3)
            pe.wait_ge(s_r, 23)
            for t in range(NT):
                ins = nc.tensor.transpose(ps_a[1][:, t * 128:(t + 1) * 128],
                                          rt[:, t, :, :].rearrange("p b e -> p (b e)"), ident)
            ins.then_inc(s_rt, 1)
            pe.wait_ge(s_ge, 16)
            pe.wait_ge(s_gs, 2)
            pe.wait_ge(s_r, 23 + 2 * (T // 16) + 2)
            pe.wait_ge(s_ot, 4 * B)

            def mask(b, i):
                for f in range(NF0):
                    ins = mm([ps_a, ps_b][i][f // 2][:, f % 2 * T:(f % 2 + 1) * T],
                             spread[:, ds((E0 * b + 4 * f) * F0, 128)], selb[:, :], start=True, stop=True)
                ins.then_inc(s_mask, 1)

            def experts0(b, i, last=False):
                if not last:
                    mask(b + 1, 1 - i)
                pe.wait_ge(s_hm, b + 1)
                pe.wait_ge(s_h2c, b + 1)
                pe.wait_ge(s_zn, b + 1)
                for t in range(NT):
                    o = ps_pv[i][:, t * C:(t + 1) * C]
                    for f in range(NF0):
                        mm(o, hm[:, i, f, t * 128:(t + 1) * 128], wl("w2", f * C, C), start=(f == 0), stop=False)
                    mm(o, sel[:, t * 128:(t + 1) * 128], b2m[:, ds(b), :].rearrange("p a c -> p (a c)"),
                       start=False, stop=False)
                    ins = mm(o, h2c[:, i, t * 128:(t + 1) * 128], ident, start=False, stop=True)
                ins.then_inc(s_z, 1)


            def scores1(b, h):
                n, g, j = 16 * b + h, h // 4, h % 4
                if j == 0:
                    pe.wait_ge(c_st[g], 64 * (b + 1))
                ge(pe, c_clip, n - 1)
                rows_j = slice(32 * j, 32 * j + 32)
                for t in range(NT):
                    ins = mm(ps_a[h % 2][:, t * T:(t + 1) * T], stack1[rows_j, g, 0, t * 128:(t + 1) * 128],
                             stack1[rows_j, g, 1, :], start=True, stop=True)
                ins.then_inc(c_s, 1)

            def turn_exp(b, h):
                n = 16 * b + h
                pe.wait_ge(c_exp, n + 1)
                ge(pe, c_ev, n - 1)
                for k in range(NT):
                    for t in range(NT):
                        ins = nc.tensor.transpose(ps_b[h % 2][:, k * T + t * 128:k * T + (t + 1) * 128],
                                                  prob1[:, h % 2, t * T + k * 128:t * T + (k + 1) * 128], ident)
                ins.then_inc(c_pt, 1)

            def pv1(b, r):
                pe.wait_ge(c_ev, 16 * b + 4 * r + 4)
                pe.wait_ge(c_vc, 2 * b + 1 + r // 2)
                if r % 2 == 0:
                    ge(pe, c_ot, 2 * b + r // 2 - 1)
                for k in range(NT):
                    for j in range(J):
                        ins = mm(ps_pv[r // 2][32 * j:32 * j + 32, r % 2 * T:(r % 2 + 1) * T], v32[:, k, J * r + j, :],
                                 probt[:, r % 2, j, k * T:(k + 1) * T], start=(k == 0), stop=(k == NT - 1))
                ins.then_inc(c_pv, 1)

            def body1(b, ticks=range(H)):
                for u in ticks:
                    if has(b, 0):
                        scores1(b, u)
                    h, off = at(u, 4)
                    if has(b, off):
                        turn_exp(b + off, h)
                    for r, tick, off in ((0, 9, 0), (1, 13, 0), (2, 1, -1), (3, 5, -1)):
                        if u == tick and has(b, off):
                            pv1(b + off, r)
                    for p, tick, off in ((0, 2, -1), (1, 8, -1)):
                        if u == tick and has(b, off):
                            wait_emptied(pe, 1, f"t{p}", b, ORDER_1)
                            pe.wait_ge(c_ot, 2 * (b + off) + p + 1)
                            for k in range(2 * NT):
                                ins = nc.tensor.transpose(ps_m[1][:, k * 128:(k + 1) * 128],
                                                          ot1[:, p, k * 128:(k + 1) * 128], ident)
                            ins.then_inc(c_otr, 1)
                    if u == 4 and has(b, 1):
                        wait_emptied(pe, 0, "xT", b, ORDER_1)
                        pe.wait_ge(c_ln[0][4], b + 2)
                        turn(0, xn3, c_xt)
                    if u == 6 and has(b, 1):
                        wait_emptied(pe, 0, "qk", b, ORDER_1)
                        pe.wait_ge(c_ht, b + 2)
                        mm(ps_m[0][:, 0:T], wl("wq"), ht1[:, :], start=True, stop=True)
                        mm(ps_m[0][:, T:2 * T], wrec[:, 0:C], ht1[:, :], start=True, stop=True).then_inc(c_qk, 1)
                    if u == 9 and has(b, -2):
                        wait_emptied(pe, 0, "h4T", b, ORDER_1)
                        pe.wait_ge(c_ln[1][4], b - 1)
                        turn(0, xn4, c_h4p)
                    if u == 11 and has(b, 1):
                        wait_emptied(pe, 0, "v", b, ORDER_1)
                        for t in range(NT):
                            ins = mm(ps_m[0][:, t * C:(t + 1) * C], ht1[:, t * 128:(t + 1) * 128], wrec[:, C:2 * C],
                                     start=True, stop=True)
                        ins.then_inc(c_v, 1)
                    if u == 13 and has(b, -1):
                        wait_emptied(pe, 0, "oT", b, ORDER_1)
                        pe.wait_ge(c_o, b)
                        turn(0, o1, c_oT)
                    if u == 15 and has(b, -1):
                        wait_emptied(pe, 1, "y", b, ORDER_1)
                        pe.wait_ge(c_ots, b)
                        for t in range(NT):
                            ins = mm(ps_m[1][:, t * C:(t + 1) * C], o1t[:, t * 128:(t + 1) * 128], wl("wo"),
                                     start=True, stop=True)
                        ins.then_inc(c_y, 1)


            def hidden1(c, i, f2):
                ge(pe, f_ge, 9 * c + f2 - 1)
                if f2 == 0:
                    pe.wait_ge(f_xl, c + 1)
                for k in range(2):
                    cols = slice((2 * f2 + k) * 128, (2 * f2 + k + 1) * 128)
                    for wp, xp in ((0, 0), (0, 1), (1, 0)):
                        ins = mm(ps_b[(i + f2) % 2][:, k * T:(k + 1) * T], w1s[:, wp, cols], h4s[:, i, xp, :],
                                 start=(wp + xp == 0), stop=(wp == 1))
                ins.then_inc(f_h, 1)

            def logits1(lo, hi):
                for t in range(lo, hi):
                    ins = mm(ps_a[0][:, t * E1:(t + 1) * E1], h2t[:, t * 128:(t + 1) * 128], wl("router"),
                             start=False, stop=(t == B * NT - 1))
                ins.then_inc(f_lg, 1)

            def before_last1():
                pe.wait_ge(c_ev, 16 * B)
                pe.wait_ge(c_clip, 16 * B)
                pe.wait_ge(c_h4, B - 1)
                pe.wait_ge(f_w1l, 1)
                for f2 in range(NF1 // 2):
                    hidden1(0, 0, f2)
                bias_rows(wr("rb"), E1)
                logits1(0, NT * (B - 1))

            mask(0, 0)
            over_pairs(pe, experts0, body1)
            pe.wait_ge(s_zn, B + 2)

            run_loop(pe, body1, past=2, started=True, last=before_last1)

            pe.wait_ge(c_h4, B)
            logits1(NT * (B - 1), NT * B)
            for f2 in range(NF1 // 2):
                hidden1(1, 1, f2)

            pe.wait_ge(f_r, W9_STEPS)
            pe.wait_ge(c_ot, 2 * B)
            for i in range(4):
                if i >= 2:
                    pe.wait_ge(f_wtc, i - 1)
                for k in range(4):
                    ins = nc.tensor.transpose(ps_pv[i % 2][0:E1 + 1, k * 128:(k + 1) * 128], w9[:, 4 * i + k, :], ident)
                ins.then_inc(f_wt, 1)


            def second(c, i, t):
                pe.wait_ge(f_ge, 9 * c + 9)
                pe.wait_ge(f_acc, ACC_STEPS * (NT * c + t + 1))
                shared = ps_pv[t][:, 0:C]
                for f in [*range(2, NF1), 0, 1]:
                    e = (f - 2) // 2
                    o = shared if f < 2 else [ps_a, ps_m][t][e // 4][:, e % 4 * C:(e % 4 + 1) * C]
                    if f == 0:
                        pe.wait_ge(f_wtc, 4)
                    mm(o, hid[:, i, f, t * 128:(t + 1) * 128], wl("w2b", f * C, C), start=(f % 2 == 0),
                       stop=(f % 2 == 1 and f >= 2))
                pe.wait_ge(f_wc, c + 1)
                mm(shared, w9c[:, i, t * 128:(t + 1) * 128], rb2_s[:, :], start=False, stop=True).then_inc(f_se, 1)

            def chunk(c, i, last=False, ahead=True):
                for f2 in range(NF1 // 2):
                    if not last and ahead:
                        hidden1(c + 1, 1 - i, f2)
                    if f2 in (1, 5):
                        second(c, i, f2 // 4)

            chunk(0, 0, ahead=False)
            chunk(1, 1)
            with pe.Fori(1, B // 2 - 1) as pair:
                for i in range(2):
                    chunk(2 * pair + i, i)
            chunk(B - 2, 0)
            chunk(B - 1, 1, last=True)


def layout(i):
    import numpy as np
    f = {k: np.asarray(v) for k, v in i.items()}
    heads = lambda w: w.transpose(1, 0, 2).reshape(C, H * HS)
    tiles = lambda w, n: w.reshape(n, 128, -1).transpose(1, 0, 2).reshape(128, -1)
    p = np.arange(128)
    eye = np.eye(128, dtype=np.float32)
    at = np.arange(T, dtype=np.float32)
    decay = np.exp(np.float32(-0.01 * 0.01) * np.abs(at[:, None] - at[None, :])) * np.float32(SCALE1)
    e = {"ct": np.concatenate([f["L0_c"].T, f["L1_c"].T], 1), "wmod0": f["L0_wmod"], "wmod1": f["L1_wmod"],
         "wqk0": np.concatenate([heads(f[f"L0_attn_{n}"]) for n in ("wq1", "wq2", "wk1", "wk2")], 1),
         "wv0": heads(f["L0_attn_wv"]), "ident": eye}
    l = {"wg": f["L0_ffn_wg"], "w1": f["L0_ffn_w1"].transpose(1, 0, 2).reshape(C, E0 * F0),
         "b1": f["L0_ffn_b1"].reshape(NF0, 128).T, "w2": tiles(f["L0_ffn_w2"].reshape(E0 * F0, C), NF0),
         "iota": np.broadcast_to(np.arange(E0, dtype=np.float32), (128, E0)),
         "blocks": (p[:, None] // E0 == np.arange(B)[None, :]).astype(np.float32),
         "wq": f["L1_attn_Wq"], "wkt": f["L1_attn_Wk"].T, "wvt": f["L1_attn_Wv"].T, "wo": f["L1_attn_Wo"],
         "wdown": f["L1_attn_W_down_kv"], "router": f["L1_ffn_router_w"],
         "w1b": np.concatenate([f["L1_ffn_sw1"], f["L1_ffn_rw1"].transpose(1, 0, 2).reshape(C, E1 * F1)], 1),
         "b1b": np.concatenate([f["L1_ffn_sb1"], f["L1_ffn_rb1"].reshape(-1)]).reshape(NF1, 128).T,
         "w2b": np.concatenate([tiles(f["L1_ffn_sw2"], 2), tiles(f["L1_ffn_rw2"].reshape(E1 * F1, C), NF1 - 2)], 1),
         "decay": tiles(decay, NT)}
    r = {"gammas": np.concatenate([f[f"L0_{n}"] for n in ("attn_ln_gamma", "attn_ln_beta", "ffn_gamma", "ffn_beta")]),
         "lamb": f["L0_attn_lamb"].reshape(1), "bg": f["L0_ffn_bg"], "rb": f["L1_ffn_router_b"]}
    pack = lambda parts, d: np.ascontiguousarray(np.concatenate([d[n].reshape(-1, k) for n, k in parts], 1))
    return {"x": np.ascontiguousarray(f["L0_attn_x"].reshape(B * NT, 128, C).transpose(1, 0, 2)),
            "early": pack(EARLY, e), "late": pack(LATE, l), "rows": pack(ROWS, r), "b2": f["L0_ffn_b2"],
            "wup": np.concatenate([f["L1_attn_W_up_k"], f["L1_attn_W_up_v"]], 1),
            "rb2": np.concatenate([f["L1_ffn_rb2"], f["L1_ffn_sb2"][None]], 0)}


def kernel(**inputs):
    import numpy as np
    import concourse.bacc as bacc
    from concourse.bass_utils import run_bass_kernel_spmd
    nc = bacc.Bacc("TRN2", target_bir_lowering=False, num_devices=1)
    arrays, args = {}, {}
    for name, a in layout(inputs).items():
        arrays[f"in_{name}"] = a
        args[name] = nc.dram_tensor(f"in_{name}", a.shape, mybir.dt.from_np(a.dtype), kind="ExternalInput").ap()
    out = nc.dram_tensor("out", (128, B * NT, C), F32, kind="ExternalOutput").ap()
    build(nc, **args, out=out)
    got = run_bass_kernel_spmd(nc, [arrays], core_ids=[0]).results[0]["out"]
    return np.ascontiguousarray(got.transpose(1, 0, 2)).reshape(B, T, C)
```
